# Optimizing a Trainium2 kernel written in Bass

```python
import numpy as np
import jax
import jax.numpy as jnp

def _softmax(x, axis=-1):
    return jax.nn.softmax(x, axis=axis)

def _gelu(x):
    return jax.nn.gelu(x, approximate=True)

def _silu(x):
    return jax.nn.silu(x)

def _sigmoid(x):
    return jax.nn.sigmoid(x)

def _layernorm(x, axis=-1, eps=1e-05):
    m = jnp.mean(x, axis=axis, keepdims=True)
    v = jnp.var(x, axis=axis, keepdims=True)
    return (x - m) / jnp.sqrt(v + eps)

def _scatter_add(tgt, idx, src, axis=0):
    return tgt.at[idx].add(src)

def _segment_sum(src, seg, n):
    return jax.ops.segment_sum(src, seg, n)
kernel_name = 'mk_gps_d2_gnn_r8_e9d775'

def setup_inputs(seed: int=0):
    np.random.seed(seed)
    _w = jnp.asarray

    def _rec_inputs():
        import jax
        import jax.numpy as jnp
        _gk = jax.random.key(seed)
        x = -0.0002117 + 1 * jax.random.normal(jax.random.fold_in(_gk, 1), (12500, 256), jnp.float32)
        src = jax.random.randint(jax.random.fold_in(_gk, 2), (200000,), 0, 12500, jnp.int32)
        dst = jnp.minimum((12500 * jax.random.uniform(jax.random.fold_in(_gk, 3), (200000,)) ** 2.0).astype(jnp.int32), 99999)
        _o = jnp.argsort(dst, stable=True)
        src = src[_o]
        dst = dst[_o]
        edge_weight = jax.random.uniform(jax.random.fold_in(_gk, 13), (200000,), jnp.float32, 0.0, 1)
        return (x, src, dst, edge_weight)
    x, src, dst, edge_weight = _rec_inputs()

    def _L0_gnn_setup():
        import jax, jax.numpy as jnp
        import numpy as np
        N_NODES = 12500
        N_EDGES = 400000
        D_IN = 256
        D_OUT = 256
        key = jax.random.key(seed)
        k1, k2, k3, k4, k5, k6 = jax.random.split(key, 6)
        bound = 1.0 / np.sqrt(D_OUT)
        x = jax.random.normal(k1, (N_NODES, D_IN), dtype=jnp.float32)
        weight = jax.random.uniform(k2, (D_IN, D_OUT), dtype=jnp.float32, minval=-bound, maxval=bound)
        bias = jax.random.uniform(k3, (D_OUT,), dtype=jnp.float32, minval=-bound, maxval=bound)
        edge_src = jax.random.randint(k4, (N_EDGES,), 0, N_NODES, dtype=jnp.int32)
        edge_dst = jax.random.randint(k5, (N_EDGES,), 0, N_NODES, dtype=jnp.int32)
        edge_weight = jax.random.uniform(k6, (N_EDGES,), dtype=jnp.float32)
        return {'x': x, 'weight': weight, 'bias': bias, 'edge_src': edge_src, 'edge_dst': edge_dst, 'edge_weight': edge_weight}
    _L0_gnn_all = _L0_gnn_setup()
    _L0_gnn_in = {k: v for k, v in _L0_gnn_all.items() if k in ('weight', 'bias')}
    del _L0_gnn_all

    def _L0_mix_setup():
        import jax, jax.numpy as jnp
        import numpy as np
        B, N, C, H = (8, 2048, 256, 8)
        D = C // H
        GH = C // 4
        key = jax.random.key(seed)
        ks = jax.random.split(key, 6)
        s = 0.02
        return {'x': jax.random.normal(ks[0], (B, N, C), dtype=jnp.float32), 'Wqkv': jax.random.normal(ks[1], (C, 3 * C), dtype=jnp.float32) * s, 'Wproj': jax.random.normal(ks[2], (C, C), dtype=jnp.float32) * s, 'bproj': jnp.zeros((C,), dtype=jnp.float32), 'ln_g': jnp.ones((C,), dtype=jnp.float32), 'ln_b': jnp.zeros((C,), dtype=jnp.float32), 'Wg1': jax.random.normal(ks[3], (C, GH), dtype=jnp.float32) * s, 'bg1': jnp.zeros((GH,), dtype=jnp.float32), 'Wg2': jax.random.normal(ks[4], (GH, C), dtype=jnp.float32) * s, 'bg2': jnp.zeros((C,), dtype=jnp.float32)}
    _L0_mix_all = _L0_mix_setup()
    _L0_mix_in = {k: v for k, v in _L0_mix_all.items() if k in ('Wqkv', 'Wproj', 'bproj', 'ln_g', 'ln_b', 'Wg1', 'bg1', 'Wg2', 'bg2')}
    del _L0_mix_all

    def _L0_ffn_setup():
        import jax, jax.numpy as jnp
        import numpy as np
        B, A = (512, 8)
        IN, OUT = (256, 256)
        SH1, SH2 = (256, 128)
        EH1, EH2 = (128, 64)
        E, TOPK = (4, 2)

        def _shared_mlp(x, W1, b1, W2, b2, W3, b3):
            h = jax.nn.relu(x @ W1 + b1)
            h = jax.nn.relu(h @ W2 + b2)
            return h @ W3 + b3

        def _experts_mlp(x, eW1, eb1, eW2, eb2, eW3, eb3):
            h = jax.nn.relu(jnp.einsum('baf,efh->ebah', x, eW1) + eb1[:, None, None, :])
            h = jax.nn.relu(jnp.einsum('ebah,ehg->ebag', h, eW2) + eb2[:, None, None, :])
            o = jnp.einsum('ebag,ego->ebao', h, eW3) + eb3[:, None, None, :]
            return jnp.moveaxis(o, 0, -1)
        key = jax.random.key(seed)
        ks = jax.random.split(key, 16)
        s = 0.05
        return {'x': jax.random.normal(ks[0], (B, A, IN), jnp.float32), 'sW1': jax.random.normal(ks[1], (IN, SH1), jnp.float32) * s, 'sb1': jnp.zeros((SH1,), jnp.float32), 'sW2': jax.random.normal(ks[2], (SH1, SH2), jnp.float32) * s, 'sb2': jnp.zeros((SH2,), jnp.float32), 'sW3': jax.random.normal(ks[3], (SH2, OUT), jnp.float32) * s, 'sb3': jnp.zeros((OUT,), jnp.float32), 'eW1': jax.random.normal(ks[4], (E, IN, EH1), jnp.float32) * s, 'eb1': jnp.zeros((E, EH1), jnp.float32), 'eW2': jax.random.normal(ks[5], (E, EH1, EH2), jnp.float32) * s, 'eb2': jnp.zeros((E, EH2), jnp.float32), 'eW3': jax.random.normal(ks[6], (E, EH2, OUT), jnp.float32) * s, 'eb3': jnp.zeros((E, OUT), jnp.float32), 'gW': jax.random.normal(ks[7], (IN, E), jnp.float32) * s, 'gb': jnp.zeros((E,), jnp.float32)}
    _L0_ffn_all = _L0_ffn_setup()
    _L0_ffn_in = {k: v for k, v in _L0_ffn_all.items() if k in ('sW1', 'sb1', 'sW2', 'sb2', 'sW3', 'sb3', 'eW1', 'eb1', 'eW2', 'eb2', 'eW3', 'eb3', 'gW', 'gb')}
    del _L0_ffn_all

    def _L1_gnn_setup():
        import jax, jax.numpy as jnp
        import numpy as np
        N, E, C, H = (1250, 40000, 256, 4)
        DH = C // H
        BN_EPS = 1e-05
        NEG_SLOPE = 0.2
        key = jax.random.key(seed)
        ks = jax.random.split(key, 16)
        s = 0.05
        return {'x': jax.random.normal(ks[0], (N, C), jnp.float32), 'edge_index': jax.random.randint(ks[1], (2, E), 0, N, jnp.int64), 'edge_weight': jax.random.uniform(ks[2], (E,), jnp.float32), 'W_gcn': jax.random.normal(ks[3], (C, C), jnp.float32) * s, 'b_gcn': jax.random.normal(ks[4], (C,), jnp.float32) * s, 'W_gat': jax.random.normal(ks[5], (C, H * DH), jnp.float32) * s, 'a_src': jax.random.normal(ks[6], (H, DH), jnp.float32) * s, 'a_dst': jax.random.normal(ks[7], (H, DH), jnp.float32) * s, 'b_gat': jax.random.normal(ks[8], (H * DH,), jnp.float32) * s, 'W_proj': jax.random.normal(ks[9], (C, C), jnp.float32) * s, 'b_proj': jax.random.normal(ks[10], (C,), jnp.float32) * s, 'bn_gamma': jax.random.uniform(ks[11], (C,), jnp.float32, 0.5, 1.5), 'bn_beta': jax.random.normal(ks[12], (C,), jnp.float32) * s, 'bn_mean': jax.random.normal(ks[13], (C,), jnp.float32) * 0.1, 'bn_var': jax.random.uniform(ks[14], (C,), jnp.float32, 0.5, 1.5)}
    _L1_gnn_all = _L1_gnn_setup()
    _L1_gnn_in = {k: v for k, v in _L1_gnn_all.items() if k in ('W_gcn', 'b_gcn', 'W_gat', 'a_src', 'a_dst', 'b_gat', 'W_proj', 'b_proj', 'bn_gamma', 'bn_beta', 'bn_mean', 'bn_var')}
    del _L1_gnn_all

    def _L1_mix_setup():
        import jax, jax.numpy as jnp
        import numpy as np
        D_MODEL = 256
        NHEAD = 8
        D_HEAD = D_MODEL // NHEAD
        DIM_FF = 1024
        B, L = (4, 2048)
        LN_EPS = 1e-05

        def _layernorm(x, g, b):
            mu = jnp.mean(x, axis=-1, keepdims=True)
            var = jnp.mean((x - mu) ** 2, axis=-1, keepdims=True)
            return (x - mu) * jax.lax.rsqrt(var + LN_EPS) * g + b

        def _phi(x):
            return jnp.where(x > 0, x + 1.0, jnp.exp(x))
        key = jax.random.key(seed)
        ks = jax.random.split(key, 16)
        s_in = 1.0 / np.sqrt(D_MODEL)
        s_ff = 1.0 / np.sqrt(DIM_FF)
        inp = {'x': jax.random.normal(ks[0], (B, L, D_MODEL), dtype=jnp.float32), 'Wq': jax.random.normal(ks[1], (D_MODEL, D_MODEL), dtype=jnp.float32) * s_in, 'bq': jnp.zeros((D_MODEL,), jnp.float32), 'Wk': jax.random.normal(ks[2], (D_MODEL, D_MODEL), dtype=jnp.float32) * s_in, 'bk': jnp.zeros((D_MODEL,), jnp.float32), 'Wv': jax.random.normal(ks[3], (D_MODEL, D_MODEL), dtype=jnp.float32) * s_in, 'bv': jnp.zeros((D_MODEL,), jnp.float32), 'Wo': jax.random.normal(ks[4], (D_MODEL, D_MODEL), dtype=jnp.float32) * s_in, 'bo': jnp.zeros((D_MODEL,), jnp.float32), 'W1': jax.random.normal(ks[5], (D_MODEL, DIM_FF), dtype=jnp.float32) * s_in, 'b1': jnp.zeros((DIM_FF,), jnp.float32), 'W2': jax.random.normal(ks[6], (DIM_FF, D_MODEL), dtype=jnp.float32) * s_ff, 'b2': jnp.zeros((D_MODEL,), jnp.float32), 'ln1_g': jnp.ones((D_MODEL,), jnp.float32), 'ln1_b': jnp.zeros((D_MODEL,), jnp.float32), 'ln2_g': jnp.ones((D_MODEL,), jnp.float32), 'ln2_b': jnp.zeros((D_MODEL,), jnp.float32)}
        return inp
    _L1_mix_all = _L1_mix_setup()
    _L1_mix_in = {k: v for k, v in _L1_mix_all.items() if k in ('Wq', 'bq', 'Wk', 'bk', 'Wv', 'bv', 'Wo', 'bo', 'W1', 'b1', 'W2', 'b2', 'ln1_g', 'ln1_b', 'ln2_g', 'ln2_b')}
    del _L1_mix_all

    def _L1_ffn_setup():
        import jax, jax.numpy as jnp
        import numpy as np
        B, S, D = (8, 512, 256)
        H = 4 * D
        CAPACITY = 0.5
        key = jax.random.key(seed)
        ks = jax.random.split(key, 6)
        x = jax.random.normal(ks[0], (B, S, D), dtype=jnp.float32)
        attention_mask = jnp.zeros((B, 1, 1, S), dtype=jnp.float32)
        wr = jax.random.normal(ks[1], (D, 1), dtype=jnp.float32) * 0.02
        br = jnp.zeros((1,), dtype=jnp.float32)
        w1 = jax.random.normal(ks[2], (D, H), dtype=jnp.float32) * 0.02
        b1 = jnp.zeros((H,), dtype=jnp.float32)
        w2 = jax.random.normal(ks[3], (H, D), dtype=jnp.float32) * 0.02
        b2 = jnp.zeros((D,), dtype=jnp.float32)
        return {'x': x, 'attention_mask': attention_mask, 'wr': wr, 'br': br, 'w1': w1, 'b1': b1, 'w2': w2, 'b2': b2}
    _L1_ffn_all = _L1_ffn_setup()
    _L1_ffn_in = {k: v for k, v in _L1_ffn_all.items() if k in ('attention_mask', 'wr', 'br', 'w1', 'b1', 'w2', 'b2')}
    del _L1_ffn_all
    return {'x': x, 'src': src, 'dst': dst, 'edge_weight': edge_weight, 'L0_gnn_weight': _L0_gnn_in['weight'], 'L0_gnn_bias': _L0_gnn_in['bias'], 'L0_mix_Wqkv': _L0_mix_in['Wqkv'], 'L0_mix_Wproj': _L0_mix_in['Wproj'], 'L0_mix_bproj': _L0_mix_in['bproj'], 'L0_mix_ln_g': _L0_mix_in['ln_g'], 'L0_mix_ln_b': _L0_mix_in['ln_b'], 'L0_mix_Wg1': _L0_mix_in['Wg1'], 'L0_mix_bg1': _L0_mix_in['bg1'], 'L0_mix_Wg2': _L0_mix_in['Wg2'], 'L0_mix_bg2': _L0_mix_in['bg2'], 'L0_ffn_sW1': _L0_ffn_in['sW1'], 'L0_ffn_sb1': _L0_ffn_in['sb1'], 'L0_ffn_sW2': _L0_ffn_in['sW2'], 'L0_ffn_sb2': _L0_ffn_in['sb2'], 'L0_ffn_sW3': _L0_ffn_in['sW3'], 'L0_ffn_sb3': _L0_ffn_in['sb3'], 'L0_ffn_eW1': _L0_ffn_in['eW1'], 'L0_ffn_eb1': _L0_ffn_in['eb1'], 'L0_ffn_eW2': _L0_ffn_in['eW2'], 'L0_ffn_eb2': _L0_ffn_in['eb2'], 'L0_ffn_eW3': _L0_ffn_in['eW3'], 'L0_ffn_eb3': _L0_ffn_in['eb3'], 'L0_ffn_gW': _L0_ffn_in['gW'], 'L0_ffn_gb': _L0_ffn_in['gb'], 'L1_gnn_W_gcn': _L1_gnn_in['W_gcn'], 'L1_gnn_b_gcn': _L1_gnn_in['b_gcn'], 'L1_gnn_W_gat': _L1_gnn_in['W_gat'], 'L1_gnn_a_src': _L1_gnn_in['a_src'], 'L1_gnn_a_dst': _L1_gnn_in['a_dst'], 'L1_gnn_b_gat': _L1_gnn_in['b_gat'], 'L1_gnn_W_proj': _L1_gnn_in['W_proj'], 'L1_gnn_b_proj': _L1_gnn_in['b_proj'], 'L1_gnn_bn_gamma': _L1_gnn_in['bn_gamma'], 'L1_gnn_bn_beta': _L1_gnn_in['bn_beta'], 'L1_gnn_bn_mean': _L1_gnn_in['bn_mean'], 'L1_gnn_bn_var': _L1_gnn_in['bn_var'], 'L1_mix_Wq': _L1_mix_in['Wq'], 'L1_mix_bq': _L1_mix_in['bq'], 'L1_mix_Wk': _L1_mix_in['Wk'], 'L1_mix_bk': _L1_mix_in['bk'], 'L1_mix_Wv': _L1_mix_in['Wv'], 'L1_mix_bv': _L1_mix_in['bv'], 'L1_mix_Wo': _L1_mix_in['Wo'], 'L1_mix_bo': _L1_mix_in['bo'], 'L1_mix_W1': _L1_mix_in['W1'], 'L1_mix_b1': _L1_mix_in['b1'], 'L1_mix_W2': _L1_mix_in['W2'], 'L1_mix_b2': _L1_mix_in['b2'], 'L1_mix_ln1_g': _L1_mix_in['ln1_g'], 'L1_mix_ln1_b': _L1_mix_in['ln1_b'], 'L1_mix_ln2_g': _L1_mix_in['ln2_g'], 'L1_mix_ln2_b': _L1_mix_in['ln2_b'], 'L1_ffn_attention_mask': _L1_ffn_in['attention_mask'], 'L1_ffn_wr': _L1_ffn_in['wr'], 'L1_ffn_br': _L1_ffn_in['br'], 'L1_ffn_w1': _L1_ffn_in['w1'], 'L1_ffn_b1': _L1_ffn_in['b1'], 'L1_ffn_w2': _L1_ffn_in['w2'], 'L1_ffn_b2': _L1_ffn_in['b2']}

def reference(x, src, dst, edge_weight, L0_gnn_weight, L0_gnn_bias, L0_mix_Wqkv, L0_mix_Wproj, L0_mix_bproj, L0_mix_ln_g, L0_mix_ln_b, L0_mix_Wg1, L0_mix_bg1, L0_mix_Wg2, L0_mix_bg2, L0_ffn_sW1, L0_ffn_sb1, L0_ffn_sW2, L0_ffn_sb2, L0_ffn_sW3, L0_ffn_sb3, L0_ffn_eW1, L0_ffn_eb1, L0_ffn_eW2, L0_ffn_eb2, L0_ffn_eW3, L0_ffn_eb3, L0_ffn_gW, L0_ffn_gb, L1_gnn_W_gcn, L1_gnn_b_gcn, L1_gnn_W_gat, L1_gnn_a_src, L1_gnn_a_dst, L1_gnn_b_gat, L1_gnn_W_proj, L1_gnn_b_proj, L1_gnn_bn_gamma, L1_gnn_bn_beta, L1_gnn_bn_mean, L1_gnn_bn_var, L1_mix_Wq, L1_mix_bq, L1_mix_Wk, L1_mix_bk, L1_mix_Wv, L1_mix_bv, L1_mix_Wo, L1_mix_bo, L1_mix_W1, L1_mix_b1, L1_mix_W2, L1_mix_b2, L1_mix_ln1_g, L1_mix_ln1_b, L1_mix_ln2_g, L1_mix_ln2_b, L1_ffn_attention_mask, L1_ffn_wr, L1_ffn_br, L1_ffn_w1, L1_ffn_b1, L1_ffn_w2, L1_ffn_b2):
    import jax
    import jax.numpy as jnp

    def _L0_gnn_ref(x, weight, bias, edge_src, edge_dst, edge_weight):
        import jax, jax.numpy as jnp
        import numpy as np
        N_NODES = 12500
        N_EDGES = 400000
        D_IN = 256
        D_OUT = 256
        xw = jnp.matmul(x, weight)
        msgs = xw[edge_src] * edge_weight[:, None]
        z = jax.ops.segment_sum(msgs, edge_dst, num_segments=N_NODES)
        return z + bias

    def _L0_mix_ref(x, Wqkv, Wproj, bproj, ln_g, ln_b, Wg1, bg1, Wg2, bg2):
        import jax, jax.numpy as jnp
        import numpy as np
        B, N, C, H = (8, 2048, 256, 8)
        D = C // H
        GH = C // 4
        b, n, c = x.shape
        h, d = (H, D)
        qkv = (x @ Wqkv).reshape(b, n, 3, h, d)
        q, k, v = (qkv[:, :, 0], qkv[:, :, 1], qkv[:, :, 2])
        k = jax.nn.softmax(k, axis=1)
        context = jnp.einsum('bnhd,bnhv->bhdv', k, v)
        out = jnp.einsum('bnhd,bhdv->bnhv', q, context).reshape(b, n, c)
        mu = jnp.mean(x, axis=-1, keepdims=True)
        var = jnp.var(x, axis=-1, keepdims=True)
        xn = (x - mu) * jax.lax.rsqrt(var + 1e-05) * ln_g + ln_b
        hgate = jax.nn.gelu(xn @ Wg1 + bg1, approximate=False)
        gate = jax.nn.sigmoid(hgate @ Wg2 + bg2)
        return out * gate @ Wproj + bproj

    def _L0_ffn_ref(x, sW1, sb1, sW2, sb2, sW3, sb3, eW1, eb1, eW2, eb2, eW3, eb3, gW, gb):
        import jax, jax.numpy as jnp
        import numpy as np
        B, A = (512, 8)
        IN, OUT = (256, 256)
        SH1, SH2 = (256, 128)
        EH1, EH2 = (128, 64)
        E, TOPK = (4, 2)

        def _shared_mlp(x, W1, b1, W2, b2, W3, b3):
            h = jax.nn.relu(x @ W1 + b1)
            h = jax.nn.relu(h @ W2 + b2)
            return h @ W3 + b3

        def _experts_mlp(x, eW1, eb1, eW2, eb2, eW3, eb3):
            h = jax.nn.relu(jnp.einsum('baf,efh->ebah', x, eW1) + eb1[:, None, None, :])
            h = jax.nn.relu(jnp.einsum('ebah,ehg->ebag', h, eW2) + eb2[:, None, None, :])
            o = jnp.einsum('ebag,ego->ebao', h, eW3) + eb3[:, None, None, :]
            return jnp.moveaxis(o, 0, -1)
        all_out = _experts_mlp(x, eW1, eb1, eW2, eb2, eW3, eb3)
        shared = _shared_mlp(x, sW1, sb1, sW2, sb2, sW3, sb3)
        gates = jax.nn.softmax(x @ gW + gb, axis=-1)
        topv, topi = jax.lax.top_k(gates, TOPK)
        topw = jax.nn.softmax(topv, axis=-1)
        sel = jnp.take_along_axis(all_out, topi[:, :, None, :], axis=-1)
        gated = jnp.sum(sel * topw[:, :, None, :], axis=-1)
        return shared + gated

    def _L1_gnn_ref(x, edge_index, edge_weight, W_gcn, b_gcn, W_gat, a_src, a_dst, b_gat, W_proj, b_proj, bn_gamma, bn_beta, bn_mean, bn_var):
        import jax, jax.numpy as jnp
        import numpy as np
        N, E, C, H = (1250, 40000, 256, 4)
        DH = C // H
        BN_EPS = 1e-05
        NEG_SLOPE = 0.2
        n = x.shape[0]
        loop = jnp.arange(n)
        src = jnp.concatenate([edge_index[0], loop])
        dst = jnp.concatenate([edge_index[1], loop])
        ew = jnp.concatenate([edge_weight, jnp.ones((n,), x.dtype)])
        deg = jax.ops.segment_sum(ew, dst, num_segments=n)
        dinv = jnp.where(deg > 0, jax.lax.rsqrt(jnp.maximum(deg, 1e-12)), 0.0)
        norm = dinv[src] * ew * dinv[dst]
        h = x @ W_gcn
        gcn_out = jax.ops.segment_sum(norm[:, None] * h[src], dst, num_segments=n) + b_gcn
        hg = (x @ W_gat).reshape(n, H, DH)
        al_src = jnp.sum(hg * a_src, axis=-1)
        al_dst = jnp.sum(hg * a_dst, axis=-1)
        e = jax.nn.leaky_relu(al_src[src] + al_dst[dst], NEG_SLOPE)
        emax = jax.ops.segment_max(e, dst, num_segments=n)
        ee = jnp.exp(e - emax[dst])
        att = ee / jax.ops.segment_sum(ee, dst, num_segments=n)[dst]
        gat = jax.ops.segment_sum(att[..., None] * hg[src], dst, num_segments=n)
        gat = gat.reshape(n, H * DH) + b_gat
        gat = gat @ W_proj + b_proj
        out = gcn_out + gat
        out = bn_gamma * (out - bn_mean) * jax.lax.rsqrt(bn_var + BN_EPS) + bn_beta
        out = jax.nn.relu(out)
        return out + x

    def _L1_mix_ref(x, Wq, bq, Wk, bk, Wv, bv, Wo, bo, W1, b1, W2, b2, ln1_g, ln1_b, ln2_g, ln2_b):
        import jax, jax.numpy as jnp
        import numpy as np
        D_MODEL = 256
        NHEAD = 8
        D_HEAD = D_MODEL // NHEAD
        DIM_FF = 1024
        B, L = (4, 2048)
        LN_EPS = 1e-05

        def _layernorm(x, g, b):
            mu = jnp.mean(x, axis=-1, keepdims=True)
            var = jnp.mean((x - mu) ** 2, axis=-1, keepdims=True)
            return (x - mu) * jax.lax.rsqrt(var + LN_EPS) * g + b

        def _phi(x):
            return jnp.where(x > 0, x + 1.0, jnp.exp(x))
        Bq, Lq, _ = x.shape
        q = (x @ Wq + bq).reshape(Bq, Lq, NHEAD, D_HEAD)
        k = (x @ Wk + bk).reshape(Bq, Lq, NHEAD, D_HEAD)
        v = (x @ Wv + bv).reshape(Bq, Lq, NHEAD, D_HEAD)
        q_phi = _phi(q)
        k_phi = _phi(k)
        kv = jnp.einsum('blhd,blhe->bhde', k_phi, v)
        k_sum = k_phi.sum(axis=1)
        z = 1.0 / (jnp.einsum('blhd,bhd->blh', q_phi, k_sum) + 1e-06)
        out = jnp.einsum('blhd,bhde,blh->blhe', q_phi, kv, z)
        out = out.reshape(Bq, Lq, D_MODEL) @ Wo + bo
        x = _layernorm(x + out, ln1_g, ln1_b)
        ff = jax.nn.relu(x @ W1 + b1) @ W2 + b2
        x = _layernorm(x + ff, ln2_g, ln2_b)
        return x

    def _L1_ffn_ref(x, attention_mask, wr, br, w1, b1, w2, b2):
        import jax, jax.numpy as jnp
        import numpy as np
        B, S, D = (8, 512, 256)
        H = 4 * D
        CAPACITY = 0.5
        b, s, d = x.shape
        weights = (jnp.einsum('bsd,do->bso', x, wr) + br)[..., 0]
        k = max(1, int(CAPACITY * s))
        kk = k - 1 if k > 1 else 1
        _, idx = jax.lax.top_k(weights, k)
        sel_idx = idx[:, :kk]
        sel = jnp.take_along_axis(x, sel_idx[:, :, None], axis=1)
        h = jax.nn.gelu(jnp.einsum('bkd,dh->bkh', sel, w1) + b1)
        y = jnp.einsum('bkh,hd->bkd', h, w2) + b2
        w_sel = jnp.take_along_axis(weights, sel_idx, axis=1)
        y = y * w_sel[..., None]
        batch_idx = jnp.arange(b)[:, None]
        processed = jnp.zeros_like(x).at[batch_idx, sel_idx].set(y)
        return processed + x
    edge_index = jnp.stack([src, dst])
    xn = _layernorm(x, axis=-1)
    x = x + _L0_gnn_ref(xn, L0_gnn_weight, L0_gnn_bias, src, dst, edge_weight) + _L0_mix_ref(xn[None], L0_mix_Wqkv, L0_mix_Wproj, L0_mix_bproj, L0_mix_ln_g, L0_mix_ln_b, L0_mix_Wg1, L0_mix_bg1, L0_mix_Wg2, L0_mix_bg2)[0]
    x = x + _L0_ffn_ref(_layernorm(x, axis=-1)[None], L0_ffn_sW1, L0_ffn_sb1, L0_ffn_sW2, L0_ffn_sb2, L0_ffn_sW3, L0_ffn_sb3, L0_ffn_eW1, L0_ffn_eb1, L0_ffn_eW2, L0_ffn_eb2, L0_ffn_eW3, L0_ffn_eb3, L0_ffn_gW, L0_ffn_gb)[0]
    xn = _layernorm(x, axis=-1)
    x = x + _L1_gnn_ref(xn, edge_index, edge_weight, L1_gnn_W_gcn, L1_gnn_b_gcn, L1_gnn_W_gat, L1_gnn_a_src, L1_gnn_a_dst, L1_gnn_b_gat, L1_gnn_W_proj, L1_gnn_b_proj, L1_gnn_bn_gamma, L1_gnn_bn_beta, L1_gnn_bn_mean, L1_gnn_bn_var) + _L1_mix_ref(xn[None], L1_mix_Wq, L1_mix_bq, L1_mix_Wk, L1_mix_bk, L1_mix_Wv, L1_mix_bv, L1_mix_Wo, L1_mix_bo, L1_mix_W1, L1_mix_b1, L1_mix_W2, L1_mix_b2, L1_mix_ln1_g, L1_mix_ln1_b, L1_mix_ln2_g, L1_mix_ln2_b)[0]
    x = x + _L1_ffn_ref(_layernorm(x, axis=-1)[None], L1_ffn_attention_mask, L1_ffn_wr, L1_ffn_br, L1_ffn_w1, L1_ffn_b1, L1_ffn_w2, L1_ffn_b2)[0]
    return x

_drawn_inputs = setup_inputs


def setup_inputs(seed=0):
    import zlib

    import numpy as np

    out = dict(_drawn_inputs(seed))
    spreads = {'L0_mix_bproj': (0.0, 0.8),
     'L0_mix_ln_g': (1.0, 0.6),
     'L0_mix_ln_b': (0.0, 0.8),
     'L0_mix_bg1': (0.0, 0.8),
     'L0_mix_bg2': (0.0, 0.8),
     'L0_ffn_sb1': (0.0, 2.0),
     'L0_ffn_sb2': (0.0, 1.87),
     'L0_ffn_sb3': (0.0, 0.8),
     'L0_ffn_eb1': (0.0, 2.0),
     'L0_ffn_eb2': (0.0, 2.0),
     'L0_ffn_eb3': (0.0, 0.8),
     'L0_ffn_gb': (0.0, 2.0),
     'L1_mix_bq': (0.0, 2.0),
     'L1_mix_bk': (0.0, 2.0),
     'L1_mix_bv': (0.0, 0.8),
     'L1_mix_bo': (0.0, 1.168),
     'L1_mix_b1': (0.0, 1.457),
     'L1_mix_b2': (0.0, 1.071),
     'L1_mix_ln1_g': (1.0, 0.6),
     'L1_mix_ln1_b': (0.0, 0.8),
     'L1_mix_ln2_g': (1.0, 0.6),
     'L1_mix_ln2_b': (0.0, 0.822),
     'L1_ffn_b1': (0.0, 0.8),
     'L1_ffn_b2': (0.0, 0.8)}
    factors = {'L0_mix_Wqkv': 8.0,
     'L0_mix_Wproj': 8.0,
     'L0_mix_Wg1': 8.0,
     'L0_mix_Wg2': 8.0,
     'L1_gnn_b_gcn': 27.663,
     'L1_gnn_a_src': 36.425,
     'L1_gnn_a_dst': 64.0,
     'L1_gnn_b_gat': 58.928,
     'L1_gnn_b_proj': 33.199,
     'L1_gnn_bn_beta': 21.518,
     'L1_gnn_bn_var': 35.84,
     'L1_mix_Wq': 64.0,
     'L1_mix_Wk': 64.0,
     'L1_ffn_wr': 8.0,
     'L1_ffn_w1': 8.0,
     'L1_ffn_w2': 8.0,
     'L0_gnn_bias': 8.0,
     'L0_ffn_sW1': 3.709,
     'L0_ffn_sW2': 3.132,
     'L0_ffn_eW1': 8.0,
     'L0_ffn_eW2': 6.773,
     'L0_ffn_gW': 5.83,
     'L1_gnn_W_gcn': 6.335,
     'L1_gnn_W_gat': 5.8,
     'L1_gnn_W_proj': 4.316,
     'L1_gnn_bn_gamma': 8.0,
     'L1_gnn_bn_mean': 8.0,
     'L1_mix_Wv': 8.0,
     'L1_mix_Wo': 6.351}
    for name, (base, spread) in spreads.items():
        noise = np.random.default_rng([zlib.crc32(name.encode()), seed]).standard_normal(out[name].shape)
        drawn = base * np.exp(spread * noise) if base else spread * noise
        out[name] = jnp.asarray(drawn.astype(out[name].dtype))
    for name, factor in factors.items():
        out[name] = (out[name] * factor).astype(out[name].dtype)
    return out
```

```python
from contextlib import ExitStack, contextmanager

import numpy as np
import concourse.bass as bass
from concourse import mybir

F32 = mybir.dt.float32
I32 = mybir.dt.int32
U16 = mybir.dt.uint16
BF16 = mybir.dt.bfloat16
U32 = mybir.dt.uint32
ALU = mybir.AluOpType
ACT = mybir.ActivationFunctionType
AX = mybir.AxisListType.X

P = 128
NODES = 12500
C = 256
KC = C // P
EDGES = 200000
NODE_BLOCKS = -(-NODES // P)
TILES = 100
PAD_NODES = TILES * P
GROUP = 2
GROUPS = TILES // GROUP
PAIRS = GROUPS // 2
ROWS = GROUP * P
FULL_TILES = NODES // P
TAIL = NODES - FULL_TILES * P
EDGE_TILES = -(-EDGES // P)
EDGE_TAIL = EDGES - (EDGE_TILES - 1) * P
PAD_EDGES = EDGE_TILES * P
PER = EDGE_TILES
ITEMS = EDGE_TILES + NODE_BLOCKS - 1
ITEM_GROUPS = -(-ITEMS // P)
TILE_GROUPS = -(-EDGE_TILES // P)
ITEM_COLS = ITEM_GROUPS * P
BATCH = 5
RING = 10
FAR = 1 << 20
BIG = 1.0e30
EPS = 1e-5
HEADS0 = 8
GAT_HEADS = 4
GAT_D = C // GAT_HEADS
EXPERTS = 4
FF = 1024
KEEP = NODES // 2 - 1


class Phase:

    def __init__(self, nc, ctx, name):
        self.nc, self.ctx, self.name, self.sems = nc, ctx, name, []

    def sem(self, name):
        s = self.nc.alloc_semaphore(f"{self.name}_{name}")
        self.sems.append(s)
        return s

    def sb(self, name, shape, dt=F32):
        return self.ctx.enter_context(self.nc.sbuf_tensor(f"{self.name}_{name}", shape, dt))

    def psum(self, name, shape, dt=F32):
        return self.ctx.enter_context(self.nc.psum_tensor(f"{self.name}_ps_{name}", shape, dt))


@contextmanager
def phase(nc, name):
    with ExitStack() as ctx:
        ph = Phase(nc, ctx, name)
        yield ph
        nc.clear_and_free_semaphores(ph.sems)
        nc.all_engine_barrier()


def peeled(eng, count, body):
    body(0, True)
    with eng.Fori(1, count) as k:
        body(k, False)


def peeled_both(eng, count, body):
    body(0, True, False)
    with eng.Fori(1, count - 1) as k:
        body(k, False, False)
    body(count - 1, False, True)


def row(ap):
    return ap.rearrange("(a d) -> a d", a=1)


def every(ap, parts=P):
    return row(ap).to_broadcast([parts, ap.shape[0]])


def columns(ap):
    return ap.rearrange("(c p) -> p c", p=P)


def by_rows(ap):
    return ap.rearrange("(c p) n -> p c n", p=P)


def load_all(eng, sem, pairs):
    with eng.bass.allow_non_contiguous_dma(reason="bias vectors as columns"):
        for to, what in pairs:
            eng.dma_start(to, what).then_inc(sem, 16)
    return 16 * len(pairs)


BIAS_PARTS = 3


class Bias:

    def __init__(self, ph, name, width):
        self.ready, self.step = ph.sem(name + "_ready"), ph.sem(name + "_step")
        self.given = ph.sb(name + "_given", [BIAS_PARTS, width])
        self.rest = ph.sb(name + "_rest", [BIAS_PARTS, width])
        self.cut = ph.sb(name + "_cut", [BIAS_PARTS, BIAS_PARTS, width], BF16)
        self.parts = ph.sb(name + "_parts", [BIAS_PARTS, width], BF16)

    def split(self, dve, g):
        n = Count()

        def done(op):
            op.then_inc(self.step, 1)
            dve.wait_ge(self.step, n.up())

        done(dve.tensor_copy(self.rest[:, :], self.given[:, :]))
        for i in range(BIAS_PARTS):
            done(dve.tensor_copy(self.cut[:, i, :], self.rest[:, :]))
            if i < BIAS_PARTS - 1:
                done(dve.tensor_tensor(self.rest[:, :], self.rest[:, :], self.cut[:, i, :], ALU.subtract))
        done(dve.tensor_scalar(self.parts[:, :], self.cut[:, 0, :], g.ident[0:BIAS_PARTS, 0:1], None, ALU.mult))
        for i in range(1, BIAS_PARTS):
            done(dve.scalar_tensor_tensor(self.parts[:, :], self.cut[:, i, :], g.ident[0:BIAS_PARTS, i:i + 1], self.parts[:, :], ALU.mult, ALU.add))
        dve.sem_inc(self.ready, 1)


def load_groups(sp, g, xt, loaded, used):
    def body(k, first):
        for u in range(2):
            if not first:
                sp.wait_ge(used, 2 * k + u - 1)
            sp.dma_start(xt[:, u, :], g.xn_turned[bass.ds(2 * k + u, 1), :, :].rearrange("o p c -> (o p) c")).then_inc(loaded[u], 16)
    peeled(sp, PAIRS, body)


def chunk(xt, u, c, j=None):
    at = c * ROWS if j is None else c * ROWS + j * P
    return xt[:, u, at:at + (ROWS if j is None else P)]


class Count:

    def __init__(self, start=0):
        self.n = start

    def up(self, by=1):
        self.n = self.n + by
        return self.n


def col(t, i, w=1):
    return t[:, bass.ds(i * w, w)]


def load_inputs(nc, g):
    with phase(nc, "load") as ph:
        x_loaded, pads_set, zeroed = ph.sem("x_loaded"), ph.sem("pads_set"), ph.sem("zeroed")
        iotas, step, copied = ph.sem("iotas"), ph.sem("step"), ph.sem("copied")
        iota_i = ph.sb("iota_i", [P, P], I32)
        part_i = ph.sb("part_i", [P, 1], I32)
        tile_i = ph.sb("tile_i", [P, TILES], I32)
        head_i = ph.sb("head_i", [P, P], I32)
        head_f = ph.sb("head_f", [P, P])
        own_i = ph.sb("own_i", [P, 1], I32)
        own_f = ph.sb("own_f", [P, 1])
        half_i = ph.sb("half_i", [P, 2, P], I32)
        pad_dst = ph.sb("pad_dst", [1, P], I32)
        pad_src = ph.sb("pad_src", [1, P], I32)
        pad_w = ph.sb("pad_w", [1, P], F32)
        zeros = ph.sb("zeros", [P, 1024])
        x_tiles = g.given["x"][0:FULL_TILES * P, :].rearrange("(t p) c -> p t c", p=P)
        cuts = [0, 16, 32, 48, 64, 80, FULL_TILES]
        with nc.Block() as block:
            @block.sync
            def _(sp):
                sp.wait_ge(zeroed, 1)
                for a, b in zip(cuts[:-1:2], cuts[1::2]):
                    sp.dma_start(g.x_sb[:, a:b, :], x_tiles[:, a:b, :]).then_inc(x_loaded, 16)
                sp.dma_start(g.x_sb[0:TAIL, FULL_TILES, :], g.given["x"][FULL_TILES * P:NODES, :]).then_inc(x_loaded, 16)
                sp.wait_ge(x_loaded, 16 * len(cuts))

            @block.scalar
            def _(act):
                full = (EDGE_TILES - 1) * P
                for a, b in zip(cuts[1:-1:2], cuts[2::2]):
                    act.dma_start(g.x_sb[:, a:b, :], x_tiles[:, a:b, :]).then_inc(x_loaded, 16)
                for to, what in ((g.srcP, g.given["src"]), (g.dstP, g.given["dst"]), (g.wP, g.given["edge_weight"])):
                    act.dma_start(to[0:EDGE_TILES - 1, :], what[0:full].rearrange("(t p) -> t p", p=P)).then_inc(copied, 16)
                    act.dma_start(to[EDGE_TILES - 1:EDGE_TILES, 0:EDGE_TAIL],
                                  what[full:EDGES].rearrange("(t p) -> t p", t=1)).then_inc(copied, 16)
                act.wait_ge(pads_set, 4)
                for to, pad in ((g.srcP, pad_src), (g.dstP, pad_dst), (g.wP, pad_w)):
                    act.dma_start(to[EDGE_TILES - 1:EDGE_TILES, EDGE_TAIL:P], pad[:, EDGE_TAIL:P]).then_inc(copied, 16)
                n = 9
                for table in (g.dst_terms, g.max_terms):
                    flat = table.rearrange("(p a) c -> p (a c)", p=P)
                    width = flat.shape[1]
                    for a in range(0, width, 1024):
                        b = min(a + 1024, width)
                        act.dma_start(flat[:, a:b], zeros[:, 0:b - a]).then_inc(copied, 16)
                        n += 1
                act.wait_ge(copied, 16 * n)

            @block.gpsimd
            def _(pool):
                pool.iota(iota_i[:, :], pattern=[[1, P]], base=0, channel_multiplier=0).then_inc(iotas, 1)
                pool.iota(part_i[:, :], pattern=[[0, 1]], base=0, channel_multiplier=1).then_inc(iotas, 1)
                pool.iota(tile_i[:, :], pattern=[[P, TILES]], base=0, channel_multiplier=0).then_inc(iotas, 1)
                pool.iota(head_i[:, :], pattern=[[1, P // 32], [0, 32]], base=0, channel_multiplier=0).then_inc(iotas, 1)
                pool.iota(half_i[:, :, :].rearrange("p q c -> p (q c)"), pattern=[[2, 2], [1, 2], [0, 64]], base=0, channel_multiplier=0).then_inc(iotas, 1)
                pool.memset(g.ones[:, :], 1.0).then_inc(iotas, 1)
                pool.memset(g.ones_bf[:, :], 1.0).then_inc(iotas, 1)
                pool.memset(g.zrow[:, :], 0.0).then_inc(iotas, 1)
                pool.memset(g.zrow_bf[:, :], 0.0).then_inc(iotas, 1)

            @block.vector
            def _(dve):
                n = Count()
                dve.memset(g.x_sb[:, FULL_TILES:TILES, :], 0.0).then_inc(zeroed, 1)
                dve.memset(pad_dst[:, :], FAR).then_inc(pads_set, 1)
                dve.memset(pad_src[:, :], 0).then_inc(pads_set, 1)
                dve.memset(pad_w[:, :], 0.0).then_inc(pads_set, 1)
                dve.memset(zeros[:, :], 0.0).then_inc(pads_set, 1)
                dve.wait_ge(iotas, 9)
                dve.tensor_copy(g.iota[:, :], iota_i[:, :]).then_inc(step, 1)
                dve.tensor_copy(g.part[:, :], part_i[:, :]).then_inc(step, 1)
                dve.tensor_copy(g.node0[:, :], tile_i[:, :]).then_inc(step, 1)
                dve.tensor_copy(head_f[:, :], head_i[:, :]).then_inc(step, 1)
                dve.tensor_copy(g.half[:, :, :], half_i[:, :, :]).then_inc(step, 1)
                dve.tensor_scalar(own_i[:, :], part_i[:, :], 5, None, ALU.arith_shift_right).then_inc(step, 1)
                dve.wait_ge(step, n.up(6))
                dve.tensor_copy(own_f[:, :], own_i[:, :]).then_inc(step, 1)
                dve.wait_ge(step, n.up())
                dve.tensor_scalar(g.same_head[:, :], head_f[:, :], own_f[:, 0:1], None, ALU.is_equal)
                dve.tensor_scalar(g.half[:, :, :], g.half[:, :, :], g.part[:, 0:1], None, ALU.is_equal)
                dve.tensor_scalar(g.ident[:, :], g.iota[:, :], g.part[:, 0:1], None, ALU.is_equal)
                dve.tensor_scalar(g.upper[:, :], g.iota[:, :], g.part[:, 0:1], None, ALU.is_gt)
                dve.tensor_scalar(g.maskcol[:, :], g.node0[:, :], g.part[:, 0:1], float(NODES), ALU.add, ALU.is_lt).then_inc(step, 1)
                dve.wait_ge(step, n.up())
                dve.tensor_scalar(g.maskbias[:, :], g.maskcol[:, :], 1.0, BIG, ALU.subtract, ALU.mult)


def item_tables(nc, g):
    with phase(nc, "items") as ph:
        last_loaded, preset, step = ph.sem("last_loaded"), ph.sem("preset"), ph.sem("step")
        counted, summed, iotas, rows_ready = ph.sem("counted"), ph.sem("summed"), ph.sem("iotas"), ph.sem("rows_ready")
        gathered = ph.sem("gathered")
        tables, turned, kept = ph.sem("tables"), ph.sem("turned"), ph.sem("kept")
        last_i = ph.sb("last_i", [P, TILE_GROUPS], I32)
        last = ph.sb("last", [P, TILE_GROUPS])
        cnt = ph.sb("cnt", [P, NODE_BLOCKS + 1])
        starts = ph.sb("starts", [P, NODE_BLOCKS + 1])
        blocks_i = ph.sb("blocks_i", [P, NODE_BLOCKS + 1], I32)
        blocks = ph.sb("blocks", [P, NODE_BLOCKS + 1])
        item_i = ph.sb("item_i", [P, ITEM_GROUPS], I32)
        item = ph.sb("item", [P, ITEM_GROUPS])
        junk = ph.sb("junk", [P, NODE_BLOCKS + 1])
        block_of = ph.sb("block_of", [P, ITEM_GROUPS])
        base_of = ph.sb("base_of", [P, ITEM_GROUPS])
        tile_f = ph.sb("tile_f", [P, ITEM_GROUPS])
        is_first = ph.sb("is_first", [P, ITEM_GROUPS])
        code = ph.sb("code", [P, ITEM_GROUPS], I32)
        code_ready, code_moved = ph.sem("code_ready"), ph.sem("code_moved")
        tile_of = g.tile_of
        rs = ph.sb("rs", [P, ITEM_COLS], I32)
        rd = ph.sb("rd", [P, ITEM_COLS], I32)
        rf = ph.sb("rf", [P, 3, ITEM_COLS])
        ps = ph.psum("ps", [P, 512])
        pt = ph.psum("pt", [P, 2, 512])
        T = TILE_GROUPS
        tail = EDGE_TILES - 1 - (T - 1) * P
        with nc.Block() as block:
            @block.sync
            def _(sp):
                sp.wait_ge(preset, 1)
                with nc.allow_non_contiguous_dma(reason="one word of each edge tile"):
                    sp.dma_start(last_i[:, 0:T - 1], g.dstP[0:(T - 1) * P, P - 1:P].rearrange("(g p) o -> p (g o)", p=P)).then_inc(last_loaded, 16)
                    sp.dma_start(last_i[0:tail, T - 1:T], g.dstP[(T - 1) * P:EDGE_TILES - 1, P - 1:P]).then_inc(last_loaded, 16)
                    sp.wait_ge(code_ready, 1)
                    sp.dma_start(g.code_row.rearrange("(g p) -> p g", p=P), code[:, :]).then_inc(code_moved, 16)
                sp.wait_ge(code_moved, 16)
                sp.dma_start(g.item_code[:, :], g.code_row.rearrange("(a n) -> a n", a=1)).then_inc(code_moved, 16)
                sp.wait_ge(code_moved, 32)

            @block.gpsimd
            def _(pool):
                pool.iota(blocks_i[:, :], pattern=[[P, NODE_BLOCKS + 1]], base=0, channel_multiplier=0).then_inc(iotas, 1)
                pool.iota(item_i[:, :], pattern=[[P, ITEM_GROUPS]], base=0, channel_multiplier=1).then_inc(iotas, 1)
                pool.wait_ge(rows_ready, 1)
                for k in range(ITEM_GROUPS):
                    for to, what in ((rs, g.srcP), (rd, g.dstP), (rf[:, 2, :], g.wP)):
                        at = to[:, k * P:(k + 1) * P]
                        pool.indirect_dma_start(at, None, what, bass.IndirectOffsetOnAxis(tile_of[:, k:k + 1], 0)).then_inc(gathered, 16)
                pool.wait_ge(gathered, 16 * 3 * ITEM_GROUPS)

            @block.vector
            def _(dve):
                n = Count()
                dve.memset(last_i[:, :], FAR).then_inc(preset, 1)
                dve.memset(cnt[:, :], 0.0).then_inc(step, 1)
                dve.wait_ge(iotas, 2)
                dve.tensor_copy(blocks[:, :], blocks_i[:, :]).then_inc(step, 1)
                dve.tensor_copy(item[:, :], item_i[:, :]).then_inc(step, 1)
                dve.wait_ge(last_loaded, 32)
                dve.tensor_copy(last[:, :], last_i[:, :]).then_inc(step, 1)
                dve.wait_ge(step, n.up(4))
                for k in range(T):
                    dve.scalar_tensor_tensor(cnt[:, :], blocks[:, :], last[:, k:k + 1], cnt[:, :], ALU.is_gt, ALU.add).then_inc(step, 1)
                    dve.wait_ge(step, n.up())
                dve.tensor_copy(cnt[:, 0:1], cnt[:, 0:1]).then_inc(counted, 1)
                dve.wait_ge(summed, 1)
                dve.scalar_tensor_tensor(starts[:, :], blocks[:, :], 1.0 / P, ps[:, 0:NODE_BLOCKS + 1], ALU.mult, ALU.add).then_inc(step, 1)
                dve.wait_ge(step, n.up())
                for k in range(ITEM_GROUPS):
                    dve.tensor_scalar(junk[:, 0:NODE_BLOCKS], starts[:, 0:NODE_BLOCKS], item[:, k:k + 1], 0.0, ALU.is_equal, ALU.add,
                                      accum_out=is_first[:, k:k + 1]).then_inc(step, 1)
                    dve.wait_ge(step, n.up())
                for k in range(ITEM_GROUPS):
                    dve.tensor_scalar(junk[:, 0:NODE_BLOCKS - 1], starts[:, 1:NODE_BLOCKS], item[:, k:k + 1], 0.0, ALU.is_le, ALU.add,
                                      accum_out=block_of[:, k:k + 1]).then_inc(step, 1)
                    dve.wait_ge(step, n.up())
                dve.scalar_tensor_tensor(code[:, :], block_of[:, :], 2.0, is_first[:, :], ALU.mult, ALU.add).then_inc(code_ready, 1)
                dve.tensor_tensor(tile_f[:, :], item[:, :], block_of[:, :], ALU.subtract).then_inc(step, 1)
                dve.wait_ge(step, n.up())
                dve.tensor_scalar(tile_of[:, :], tile_f[:, :], float(EDGE_TILES - 1), None, ALU.min).then_inc(rows_ready, 1)
                dve.tensor_scalar(base_of[:, :], block_of[:, :], float(P), None, ALU.mult).then_inc(step, 1)
                dve.wait_ge(gathered, 16 * 3 * ITEM_GROUPS)
                dve.wait_ge(step, n.up())
                for k in range(ITEM_GROUPS):
                    at = slice(k * P, (k + 1) * P)
                    dve.tensor_copy(rf[:, 0, at], rs[:, at])
                    last_op = dve.tensor_scalar(rf[:, 1, at], rd[:, at], base_of[:, k:k + 1], None, ALU.subtract)
                last_op.then_inc(tables, 1)
                for k in range(ITEM_GROUPS):
                    at = slice(k * P, (k + 1) * P)
                    dve.wait_ge(turned, k + 1)
                    dve.tensor_copy(g.src_item[:, at], pt[:, k % 2, 0:P])
                    dve.tensor_copy(g.dst_item[:, at], pt[:, k % 2, P:2 * P])
                    dve.tensor_copy(g.w_item[:, at], pt[:, k % 2, 2 * P:3 * P]).then_inc(kept, 1)

            @block.tensor
            def _(pe):
                pe.wait_ge(counted, 1)
                pe.matmul(ps[:, 0:NODE_BLOCKS + 1], g.ones[:, :], cnt[:, :], start=True, stop=True).then_inc(summed, 1)
                pe.wait_ge(tables, 1)
                for k in range(ITEM_GROUPS):
                    if k >= 2:
                        pe.wait_ge(kept, k - 1)
                    for j in range(3):
                        mm = pe.transpose(pt[:, k % 2, j * P:(j + 1) * P], rf[:, j, k * P:(k + 1) * P], g.ident[:, :])
                    mm.then_inc(turned, 1)


def normalize(nc, g, name, rows_to=None, turned_to=None, second=None, narrow=None, add_back=False):
    SLOTS = 5
    assert GROUPS % SLOTS == 0
    with phase(nc, name) as ph:
        stats_done, step, var_ready = ph.sem("stats_done"), ph.sem("step"), ph.sem("var_ready")
        root_ready, scaled = ph.sem("root_ready"), ph.sem("scaled")
        turned, kept = ph.sem("turned"), ph.sem("kept")
        rows_out = [ph.sem(f"rows_out{u}") for u in range(SLOTS)]
        turned_out = [ph.sem(f"turned_out{u}") for u in range(SLOTS)]
        stats = ph.sb("stats", [P, TILES, 6])
        mean = ph.sb("mean", [P, TILES])
        var = ph.sb("var", [P, TILES])
        tmp = ph.sb("tmp", [P, TILES])
        root = ph.sb("root", [P, TILES])
        rstd = ph.sb("rstd", [P, TILES])
        xn = ph.sb("xn", [P, SLOTS, GROUP, C])
        xt = ph.sb("xt", [P, SLOTS, KC, ROWS])
        pt = [ph.psum(f"pt{u}", [P, KC, ROWS]) for u in range(SLOTS)]
        narrow_loaded, narrow_done, added_back = ph.sem("narrow_loaded"), ph.sem("narrow_done"), ph.sem("added_back")
        if narrow is not None:
            w_dram, narrow_out = narrow
            width = narrow_out.shape[2]
            w_sb = ph.sb("w_sb", [P, KC, width])
            ps_narrow = ph.psum("narrow", [P, 512])
        with nc.Block() as block:
            @block.vector
            def _(dve):
                n = Count()
                with dve.Fori(0, TILES) as t:
                    dve.bn_stats(stats[:, bass.ds(t, 1), :].rearrange("p o c -> p (o c)"),
                                 g.x_sb[:, bass.ds(t, 1), :].rearrange("p o c -> p (o c)")).then_inc(stats_done, 1)
                dve.wait_ge(stats_done, TILES)
                dve.tensor_tensor(mean[:, :], stats[:, :, 1], stats[:, :, 4], ALU.add).then_inc(step, 1)
                dve.tensor_tensor(tmp[:, :], stats[:, :, 1], stats[:, :, 4], ALU.subtract).then_inc(step, 1)
                dve.tensor_tensor(var[:, :], stats[:, :, 2], stats[:, :, 5], ALU.add).then_inc(step, 1)
                dve.wait_ge(step, n.up(3))
                dve.tensor_scalar(mean[:, :], mean[:, :], 0.5, None, ALU.mult).then_inc(step, 1)
                dve.tensor_tensor(tmp[:, :], tmp[:, :], tmp[:, :], ALU.mult).then_inc(step, 1)
                dve.wait_ge(step, n.up(2))
                dve.scalar_tensor_tensor(var[:, :], tmp[:, :], C / 4.0, var[:, :], ALU.mult, ALU.add).then_inc(step, 1)
                dve.wait_ge(step, n.up())
                dve.tensor_scalar(var[:, :], var[:, :], 1.0 / C, None, ALU.mult).then_inc(step, 1)
                dve.wait_ge(step, n.up())
                dve.tensor_scalar(tmp[:, :], var[:, :], EPS, None, ALU.add).then_inc(var_ready, 1)
                dve.wait_ge(root_ready, 1)
                dve.reciprocal(rstd[:, :], root[:, :]).then_inc(step, 1)
                dve.wait_ge(step, n.up())
                if second is not None:
                    dve.tensor_tensor(var[:, :], var[:, :], rstd[:, :], ALU.mult).then_inc(step, 1)
                    dve.wait_ge(step, n.up())
                    dve.tensor_tensor(var[:, :], var[:, :], rstd[:, :], ALU.mult).then_inc(step, 1)
                    dve.wait_ge(step, n.up())
                    dve.tensor_scalar(tmp[:, :], var[:, :], EPS, None, ALU.add).then_inc(var_ready, 1)
                    dve.wait_ge(root_ready, 2)
                    dve.reciprocal(second[:, :], root[:, :])

                def body(k, first):
                    for u in range(SLOTS):
                        if not first:
                            dve.wait_ge(turned, SLOTS * k + u + 1 - SLOTS)
                            if rows_to is not None:
                                dve.wait_ge(rows_out[u], 16 * k)
                            if add_back:
                                dve.wait_ge(added_back, SLOTS * k + u + 1 - SLOTS)
                        for j in range(GROUP):
                            t = (SLOTS * k + u) * GROUP + j
                            op = dve.tensor_scalar(xn[:, u, j, :], g.x_sb[:, bass.ds(t, 1), :].rearrange("p o c -> p (o c)"),
                                                   col(mean, t), col(rstd, t), ALU.subtract, ALU.mult)
                        op.then_inc(scaled, 1)
                peeled(dve, GROUPS // SLOTS, body)
                if narrow is not None:
                    dve.wait_ge(narrow_done, GROUPS)
                    dve.tensor_copy(narrow_out[:, :, :].rearrange("p t w -> p (t w)"), ps_narrow[:, 0:TILES * width])

            @block.gpsimd
            def _(pool):
                def body(k, first):
                    for u in range(SLOTS):
                        gi = SLOTS * k + u
                        pool.wait_ge(scaled, gi + 1)
                        at = g.x_sb[:, bass.ds(gi * GROUP, GROUP), :]
                        pool.tensor_tensor(at, at, xn[:, u, :, :], ALU.add).then_inc(added_back, 1)
                if add_back:
                    peeled(pool, GROUPS // SLOTS, body)

            @block.scalar
            def _(act):
                act.wait_ge(var_ready, 1)
                act.activation(root[:, :], tmp[:, :], ACT.Sqrt).then_inc(root_ready, 1)
                if second is not None:
                    act.wait_ge(var_ready, 2)
                    act.activation(root[:, :], tmp[:, :], ACT.Sqrt).then_inc(root_ready, 1)

                def body(k, first):
                    for u in range(SLOTS):
                        if not first:
                            act.wait_ge(turned_out[u], 16 * k)
                            if narrow is not None:
                                act.wait_ge(narrow_done, SLOTS * k + u + 1 - SLOTS)
                        act.wait_ge(turned, SLOTS * k + u + 1)
                        act.activation(xt[:, u, :, :], pt[u][:, :, :], ACT.Copy).then_inc(kept, 1)
                peeled(act, GROUPS // SLOTS, body)

            @block.tensor
            def _(pe):
                def few(gi, u):
                    pe.wait_ge(kept, gi + 1)
                    for j in range(GROUP):
                        for c in range(KC):
                            mm = pe.matmul(ps_narrow[:, bass.ds((gi * GROUP + j) * width, width)],
                                           xt[:, u, c, j * P:(j + 1) * P], w_sb[:, c, :], start=(c == 0), stop=(c == KC - 1))
                    mm.then_inc(narrow_done, 1)

                if narrow is not None:
                    pe.wait_ge(narrow_loaded, 16)

                def body(k, first):
                    for u in range(SLOTS):
                        pe.wait_ge(scaled, SLOTS * k + u + 1)
                        if not first:
                            pe.wait_ge(kept, SLOTS * k + u + 1 - SLOTS)
                        for j in range(GROUP):
                            for c in range(KC):
                                mm = pe.transpose(pt[u][:, c, j * P:(j + 1) * P], xn[:, u, j, c * P:(c + 1) * P], g.ident[:, :])
                        mm.then_inc(turned, 1)
                        if narrow is not None and not (first and u == 0):
                            few(SLOTS * k + u - 1, (u - 1) % SLOTS)
                peeled(pe, GROUPS // SLOTS, body)
                if narrow is not None:
                    few(GROUPS - 1, SLOTS - 1)

            @block.sync
            def _(sp):
                if narrow is not None:
                    load_all(sp, narrow_loaded, [(w_sb[:, :, :], by_rows(w_dram))])

                def body(k, first):
                    for u in range(SLOTS):
                        gi = SLOTS * k + u
                        if rows_to is not None:
                            sp.wait_ge(scaled, gi + 1)
                            sp.dma_start(rows_to[bass.ds(gi * ROWS, ROWS), :].rearrange("(j p) c -> p j c", p=P),
                                         xn[:, u, :, :]).then_inc(rows_out[u], 16)
                        sp.wait_ge(kept, gi + 1)
                        sp.dma_start(turned_to[bass.ds(gi, 1), :, :].rearrange("o p c -> (o p) c"),
                                     xt[:, u, :, :].rearrange("p c r -> p (c r)")).then_inc(turned_out[u], 16)
                peeled(sp, GROUPS // SLOTS, body)
                for u in range(SLOTS):
                    if rows_to is not None:
                        sp.wait_ge(rows_out[u], 16 * (GROUPS // SLOTS))
                    sp.wait_ge(turned_out[u], 16 * (GROUPS // SLOTS))


def aggregate0(nc, g):
    SLOTS = 2 * RING
    with phase(nc, "agg0") as ph:
        staged, landed = ph.sem("staged"), [ph.sem(f"landed{u}") for u in range(SLOTS)]
        sel_ready, item_used = ph.sem("sel_ready"), ph.sem("item_used")
        ones_set, w_loaded = ph.sem("ones_set"), ph.sem("w_loaded")
        sum_ready, sum_kept, turned, turn_kept, new_ready, new_kept = (
            ph.sem(s) for s in ("sum_ready", "sum_kept", "turned", "turn_kept", "new_ready", "new_kept"))
        issued = ph.sem("issued")
        stage = ph.sb("stage", [P, SLOTS], U32)
        rows = ph.sb("rows", [P, SLOTS, C + 1])
        sel_w = ph.sb("sel_w", [P, SLOTS, P])
        sel = ph.sb("sel", [P, SLOTS, P], BF16)
        w_sb = ph.sb("w_sb", [P, KC, C])
        bias = Bias(ph, "bias", C)
        z_sb = ph.sb("z_sb", [P, C])
        zt_sb = ph.sb("zt_sb", [P, C])
        BANK = 512
        ps_sum = ph.psum("sum", [P, 2 * BANK])
        ps_turn = ph.psum("turn", [P, C])
        ps_new = ph.psum("new", [P, C])
        W = C + 2
        STEPS = ITEMS // SLOTS
        assert STEPS * SLOTS == ITEMS
        with nc.Block() as block:
            @block.gpsimd
            def _(pool):
                pool.memset(rows[:, :, C:C + 1], 1.0).then_inc(ones_set, 1)

                def body(k, first):
                    for u in range(SLOTS):
                        i = k * SLOTS + u
                        if u % BATCH == 0:
                            if not first:
                                pool.wait_ge(item_used, i + BATCH - SLOTS)
                            pool.tensor_copy(stage[:, u:u + BATCH], g.src_item[:, bass.ds(i, BATCH)]).then_inc(staged, 1)
                            pool.wait_ge(staged, k * (SLOTS // BATCH) + u // BATCH + 1)
                            pool.sem_inc(issued, 1)
                            pool.wait_ge(ones_set, 1)
                        pool.indirect_dma_start(rows[:, u, 0:C], None, g.xn_rows,
                                                bass.IndirectOffsetOnAxis(stage[:, u:u + 1], 0)).then_inc(landed[u], 16)
                peeled(pool, STEPS, body)

            @block.sync
            def _(sp):
                sp.dma_start(w_sb[:, :, :], g.given["L0_gnn_weight"].rearrange("(c p) n -> p c n", p=P)).then_inc(w_loaded, 16)
                sp.dma_start(bias.given[:, :], every(g.given["L0_gnn_bias"], BIAS_PARTS)).then_inc(w_loaded, 16)

            @block.vector
            def _(dve):
                dve.wait_ge(w_loaded, 32)
                bias.split(dve, g)

                def body(k, first):
                    for u in range(SLOTS):
                        i = k * SLOTS + u
                        if not first and u % BATCH == 0:
                            dve.wait_ge(item_used, i + BATCH - SLOTS)
                        dve.wait_ge(landed[u], 16 * k + 16)
                        dve.tensor_scalar(sel_w[:, u, :], g.iota[:, :], col(g.dst_item, i), col(g.w_item, i), ALU.is_equal, ALU.mult)
                        dve.tensor_scalar(sel[:, u, :], g.iota[:, :], col(g.dst_item, i), None, ALU.is_equal).then_inc(sel_ready, 1)
                peeled(dve, STEPS, body)

            @block.tensor
            def _(pe):
                def open_block(bank):
                    pe.matmul(ps_sum[:, bank], g.zrow_bf[0:1, 0:P], g.zrow_bf[0:1, 0:W], start=True, stop=False)

                def end_block(bank, b):
                    pe.matmul(ps_sum[:, bank], g.zrow_bf[0:1, 0:P], g.zrow_bf[0:1, 0:W], start=False, stop=True).then_inc(sum_ready, 1)

                def turn(now):
                    pe.wait_ge(sum_kept, now)
                    pe.wait_ge(turn_kept, now)
                    for c in range(KC):
                        mm = pe.transpose(ps_turn[:, c * P:(c + 1) * P], z_sb[:, c * P:(c + 1) * P], g.ident[:, :])
                    mm.then_inc(turned, 1)

                def project(now, b):
                    pe.wait_ge(turn_kept, now)
                    pe.wait_ge(new_kept, now)
                    for c in range(KC):
                        pe.matmul(ps_new[:, :], zt_sb[:, c * P:(c + 1) * P], w_sb[:, c, :], start=(c == 0), stop=False)
                    pe.matmul(ps_new[:, :], g.ones_bf[0:BIAS_PARTS, :], bias.parts[:, :], start=False, stop=False)
                    pe.matmul(ps_new[:, :], g.ident[:, :], g.x_sb[:, bass.ds(b, 1), :].rearrange("p o c -> p (o c)"),
                              start=False, stop=True).then_inc(new_ready, 1)

                pe.wait_ge(bias.ready, 1)
                pe.wait_ge(ones_set, 1)
                open_block(slice(0, W))

                def add(u, to, count_to):
                    pe.matmul(ps_sum[:, to], sel_w[:, u, :], rows[:, u, :], start=False, stop=False, skip_group_check=True)
                    pe.matmul(ps_sum[:, count_to], sel[:, u, :], g.ones_bf[:, 0:1],
                              start=False, stop=False, skip_group_check=True).then_inc(item_used, 1)

                def one(k, u, first):
                    i = k * SLOTS + u
                    code = pe.value_load(g.item_code[0:1, bass.ds(i, 1)], min_val=0, max_val=2 * NODE_BLOCKS - 1)
                    if not (first and u == 0):
                        with pe.If(code % 2):
                            now = pe.value_load(g.item_code[0:1, bass.ds(i, 1)], min_val=3, max_val=2 * NODE_BLOCKS - 1)
                            b = pe.snap(now // 2)
                            end_block(bass.ds(((b + 1) % 2) * BANK, W), b - 1)
                            pe.wait_ge(sum_kept, b)
                            open_block(bass.ds((b % 2) * BANK, W))
                            with pe.If(b > 2):
                                far = pe.value_load(g.item_code[0:1, bass.ds(i, 1)], min_val=7, max_val=2 * NODE_BLOCKS - 1)
                                project(b, pe.snap(far // 2 - 3))
                            with pe.If(b > 1):
                                turn(b)
                    bank = (code // 2) % 2
                    pe.wait_ge(sel_ready, i + 1)
                    add(u, bass.ds(bank * BANK, C + 1), bass.ds(bank * BANK + C + 1, 1))

                def body(k, first):
                    for at in range(0, SLOTS, BATCH):
                        i = k * SLOTS + at
                        a = pe.value_load(g.item_code[0:1, bass.ds(i, 1)], min_val=0, max_val=2 * NODE_BLOCKS - 1)
                        z = pe.value_load(g.item_code[0:1, bass.ds(i + BATCH - 1, 1)], min_val=0, max_val=2 * NODE_BLOCKS - 1)
                        with pe.If(z - a):
                            for u in range(at, at + BATCH):
                                one(k, u, first)
                        with pe.Else():
                            pe.wait_ge(sel_ready, i + BATCH)
                            with pe.If((a // 2) % 2):
                                for u in range(at, at + BATCH):
                                    add(u, slice(BANK, BANK + C + 1), slice(BANK + C + 1, BANK + W))
                            with pe.Else():
                                for u in range(at, at + BATCH):
                                    add(u, slice(0, C + 1), slice(C + 1, W))
                peeled(pe, STEPS, body)
                last = NODE_BLOCKS - 1
                end_block(slice((last % 2) * BANK, (last % 2) * BANK + W), last)
                project(last + 1, last - 2)
                turn(last + 1)
                project(last + 2, last - 1)
                turn(last + 2)
                project(last + 3, last)

            @block.scalar
            def _(act):
                for kept, start in ((sum_kept, 1), (turn_kept, 2), (new_kept, 3)):
                    act.sem_inc(kept, start)

                def keep_new(b):
                    act.wait_ge(new_ready, b + 1)
                    act.activation(x_block(g, b), ps_new[:, :], ACT.Copy).then_inc(new_kept, 1)

                def keep_turn(b):
                    act.wait_ge(turned, b + 1)
                    act.activation(zt_sb[:, :], ps_turn[:, :], ACT.Copy).then_inc(turn_kept, 1)

                def keep_sum(b, u):
                    act.wait_ge(sum_ready, b + 1)
                    act.activation(z_sb[:, :], ps_sum[:, u * BANK:u * BANK + C], ACT.Copy)
                    act.activation(g.deg_cnt[:, bass.ds(b, 1), :].rearrange("p o c -> p (o c)"),
                                   ps_sum[:, u * BANK + C:u * BANK + W], ACT.Copy).then_inc(sum_kept, 1)

                keep_sum(0, 0)
                def body(k, first):
                    for u in range(2):
                        b = 2 * k + u
                        if not (first and u == 0):
                            if not (first and u == 1):
                                keep_new(b - 2)
                            keep_turn(b - 1)
                            keep_sum(b, u)
                peeled(act, NODE_BLOCKS // 2, body)
                keep_new(NODE_BLOCKS - 2)
                keep_turn(NODE_BLOCKS - 1)
                keep_new(NODE_BLOCKS - 1)


def x_block(g, b):
    return g.x_sb[:, bass.ds(b, 1), :].rearrange("p o c -> p (o c)")


def key_max(nc, g):
    FULL = NODES // ROWS
    REST = NODES - FULL * ROWS
    with phase(nc, "kmax") as ph:
        loaded, used = [ph.sem("loaded0"), ph.sem("loaded1")], ph.sem("used")
        w_loaded, reduced, step, spread = ph.sem("w_loaded"), ph.sem("reduced"), ph.sem("step"), ph.sem("spread")
        xt = ph.sb("xt", [P, 2, KC * ROWS])
        wk = ph.sb("wk", [P, KC, C])
        tops = ph.sb("tops", [P, GROUPS, KC])
        top = ph.sb("top", [P, KC])
        diag = ph.sb("diag", [P, KC, P])
        ps = [ph.psum(f"ps{u}", [P, KC, ROWS]) for u in range(2)]
        ps_row = ph.psum("row", [P, C])
        with nc.Block() as block:
            @block.sync
            def _(sp):
                load_all(sp, w_loaded, [(wk[:, :, :], by_rows(g.given["L0_mix_Wqkv"][:, C:2 * C]))])
                load_groups(sp, g, xt, loaded, used)

            @block.tensor
            def _(pe):
                pe.wait_ge(w_loaded, 16)

                def body(k, first):
                    for u in range(2):
                        pe.wait_ge(loaded[u], 16 * k + 16)
                        if not first:
                            pe.wait_ge(reduced, 2 * k + u - 1)
                        for m in range(KC):
                            for c in range(KC):
                                mm = pe.matmul(ps[u][:, m, :], wk[:, c, m * P:(m + 1) * P], chunk(xt, u, c),
                                               start=(c == 0), stop=(c == KC - 1))
                        mm.then_inc(used, 1)
                peeled(pe, PAIRS, body)
                pe.wait_ge(step, 2)
                for m in range(KC):
                    mm = pe.matmul(ps_row[:, m * P:(m + 1) * P], g.ones[:, :], diag[:, m, :], start=True, stop=True)
                mm.then_inc(spread, 1)

            @block.vector
            def _(dve):
                def body(k, first):
                    for u in range(2):
                        gi = 2 * k + u
                        dve.wait_ge(used, gi + 1)
                        dve.tensor_reduce(tops[:, bass.ds(gi, 1), :].rearrange("p o c -> p (o c)"), ps[u][:, :, :], AX, ALU.max).then_inc(reduced, 1)
                peeled(dve, FULL // 2, body)
                dve.wait_ge(used, FULL + 1)
                dve.tensor_reduce(tops[:, FULL, :], ps[0][:, :, 0:REST], AX, ALU.max).then_inc(reduced, 1)
                dve.wait_ge(reduced, FULL + 1)
                dve.tensor_reduce(top[:, :], tops[:, 0:FULL + 1, :].rearrange("p t c -> p c t"), AX, ALU.max).then_inc(step, 1)
                dve.wait_ge(step, 1)
                for m in range(KC):
                    op = dve.tensor_scalar(diag[:, m, :], g.ident[:, :], top[:, m:m + 1], None, ALU.mult)
                op.then_inc(step, 1)
                dve.wait_ge(spread, 1)
                dve.tensor_copy(g.k_shift[:, :], ps_row[:, :])


def context0(nc, g):
    with phase(nc, "ctx0") as ph:
        loaded, used = [ph.sem("loaded0"), ph.sem("loaded1")], ph.sem("used")
        w_loaded, shifted, keys_ready, step, sums_ready = (
            ph.sem(s) for s in ("w_loaded", "shifted", "keys_ready", "step", "sums_ready"))
        sums_used, q_turned, q_kept, folded, ones_set = (
            ph.sem(s) for s in ("sums_used", "q_turned", "q_kept", "folded", "ones_set"))
        xt = ph.sb("xt", [P, 2, KC * ROWS])
        wkv = ph.sb("wkv", [P, KC, 2 * C])
        wq = ph.sb("wq", [P, KC, C])
        wqt = ph.sb("wqt", [P, KC, C])
        kd = ph.sb("kd", [P, 2, GROUP, C])
        ek = ph.sb("ek", [P, 2, GROUP, C])
        v1 = ph.sb("v1", [P, 2, GROUP, KC, P + 1])
        rden = ph.sb("rden", [P, KC])
        ctx = ph.sb("ctx", [P, KC, P])
        ps = [[ph.psum(f"kv{u}{j}", [P, 2 * C]) for j in range(GROUP)] for u in range(2)]
        ps_ctx = [ph.psum(f"ctx{c}", [P, P + 1]) for c in range(KC)]
        ps_q = ph.psum("q", [P, KC, C])
        ps_fold = ph.psum("fold", [P, KC, C])
        with nc.Block() as block:
            @block.sync
            def _(sp):
                load_all(sp, w_loaded, [(wkv[:, :, :], by_rows(g.given["L0_mix_Wqkv"][:, C:3 * C])),
                                        (wq[:, :, :], by_rows(g.given["L0_mix_Wqkv"][:, 0:C]))])
                load_groups(sp, g, xt, loaded, used)

            @block.gpsimd
            def _(pool):
                pool.memset(v1[:, :, :, :, P:P + 1].rearrange("p u j c o -> p (u j c) o"), 1.0).then_inc(ones_set, 1)

            @block.tensor
            def _(pe):
                pe.wait_ge(w_loaded, 32)
                pe.wait_ge(ones_set, 1)
                for c in range(KC):
                    for d in range(KC):
                        mm = pe.transpose(ps_q[:, d, c * P:(c + 1) * P], wq[:, c, d * P:(d + 1) * P], g.ident[:, :])
                mm.then_inc(q_turned, 1)
                for c in range(KC):
                    pe.matmul(ps_ctx[c][:, :], g.zrow[0:1, 0:P], g.zrow[0:1, 0:P + 1], start=True, stop=False)

                def add(gi, u):
                    pe.wait_ge(keys_ready, gi + 1)
                    for j in range(GROUP):
                        for c in range(KC):
                            mm = pe.matmul(ps_ctx[c][:, :], ek[:, u, j, c * P:(c + 1) * P], v1[:, u, j, c, :],
                                           start=False, stop=False, skip_group_check=True)
                    mm.then_inc(sums_used, 1)

                def body(k, first):
                    for u in range(2):
                        gi = 2 * k + u
                        pe.wait_ge(loaded[u], 16 * k + 16)
                        if not first:
                            pe.wait_ge(keys_ready, gi - 1)
                        for j in range(GROUP):
                            for c in range(KC):
                                mm = pe.matmul(ps[u][j][:, :], chunk(xt, u, c, j), wkv[:, c, :], start=(c == 0), stop=(c == KC - 1))
                        mm.then_inc(used, 1)
                        if not (first and u == 0):
                            add(gi - 1, 1 - u)
                peeled(pe, PAIRS, body)
                add(GROUPS - 1, 1)
                for c in range(KC):
                    mm = pe.matmul(ps_ctx[c][:, :], g.zrow[0:1, 0:P], g.zrow[0:1, 0:P + 1], start=False, stop=True)
                mm.then_inc(sums_ready, 1)
                pe.wait_ge(step, 2 * KC)
                pe.wait_ge(q_kept, 1)
                for c in range(KC):
                    for d in range(KC):
                        mm = pe.matmul(ps_fold[:, c, d * P:(d + 1) * P], wqt[:, d, c * P:(c + 1) * P], ctx[:, d, :], start=True, stop=True)
                mm.then_inc(folded, 1)

            @block.vector
            def _(dve):
                def body(k, first):
                    for u in range(2):
                        gi = 2 * k + u
                        dve.wait_ge(used, gi + 1)
                        if not first:
                            dve.wait_ge(keys_ready, gi - 1)
                        for j in range(GROUP):
                            op = dve.tensor_tensor(kd[:, u, j, :], ps[u][j][:, 0:C], g.k_shift[:, :], ALU.subtract)
                        op.then_inc(shifted, 1)
                peeled(dve, PAIRS, body)
                dve.wait_ge(sums_ready, 1)
                for c in range(KC):
                    dve.reciprocal(rden[:, c:c + 1], ps_ctx[c][:, P:P + 1]).then_inc(step, 1)
                dve.wait_ge(step, KC)
                for c in range(KC):
                    dve.scalar_tensor_tensor(ctx[:, c, :], ps_ctx[c][:, 0:P], rden[:, c:c + 1], g.same_head[:, :], ALU.mult, ALU.mult).then_inc(step, 1)
                dve.wait_ge(folded, 1)
                dve.tensor_copy(g.wqc[:, :, :], ps_fold[:, :, :])

            @block.scalar
            def _(act):
                act.wait_ge(q_turned, 1)
                act.activation(wqt[:, :, :], ps_q[:, :, :], ACT.Copy).then_inc(q_kept, 1)

                def body(k, first):
                    for u in range(2):
                        gi = 2 * k + u
                        if not first:
                            act.wait_ge(sums_used, gi - 1)
                        act.wait_ge(shifted, gi + 1)
                        for j in range(GROUP):
                            act.activation(ek[:, u, j, :], kd[:, u, j, :], ACT.Exp, bias=col(g.maskbias, gi * GROUP + j))
                            op = act.activation(v1[:, u, j, :, 0:P], ps[u][j][:, C:2 * C].rearrange("p (c d) -> p c d", c=KC), ACT.Copy)
                        op.then_inc(keys_ready, 1)
                peeled(act, PAIRS, body)


def mix0(nc, g):
    H = C // 4
    with phase(nc, "mix0") as ph:
        loaded, used = [ph.sem("loaded0"), ph.sem("loaded1")], ph.sem("used")
        w_loaded, prepared, bias_done, step = ph.sem("w_loaded"), ph.sem("prepared"), ph.sem("bias_done"), ph.sem("step")
        scaled, bent, turned_h, kept_h, gate_done, gate_ready, gated, turned_o, kept_o, out_done, added, ones_set = (
            ph.sem(s) for s in ("scaled", "bent", "turned_h", "kept_h", "gate_done", "gate_ready", "gated",
                                "turned_o", "kept_o", "out_done", "added", "ones_set"))
        xt = ph.sb("xt", [P, 2, KC * ROWS])
        wg1 = ph.sb("wg1", [P, KC, H])
        w1 = ph.sb("w1", [P, KC, C + H])
        ln_g = ph.sb("ln_g", [P, KC])
        ln_b = ph.sb("ln_b", [P, KC])
        ln_rows = ph.sb("ln_rows", [P, KC, P])
        bg1 = ph.sb("bg1", [1, H])
        h_bias = ph.sb("h_bias", [P, H])
        wg2 = ph.sb("wg2", [H + 1, C])
        wp = ph.sb("wp", [P, KC, C])
        bp = ph.sb("bp", [1, C])
        hs = ph.sb("hs", [P, 2, GROUP, H])
        hg = ph.sb("hg", [P, 2, GROUP, P])
        ht = ph.sb("ht", [H + 1, 2, ROWS])
        gate = ph.sb("gate", [P, GROUP, C])
        prod = ph.sb("prod", [P, GROUP, C])
        pt = ph.sb("pt", [P, KC, ROWS])
        ps_a = [[ph.psum(f"a{u}{j}", [P, C + H]) for j in range(GROUP)] for u in range(2)]
        ps_b = ph.psum("b", [P, ROWS])
        ps_c = ph.psum("c", [P, GROUP, C])
        ps_d = ph.psum("d", [P, KC, ROWS])
        ps_e = ph.psum("e", [P, GROUP, C])
        with nc.Block() as block:
            @block.sync
            def _(sp):
                load_all(sp, w_loaded, [
                    (wg1[:, :, :], by_rows(g.given["L0_mix_Wg1"])), (ln_g[:, :], columns(g.given["L0_mix_ln_g"])), (ln_b[:, :], columns(g.given["L0_mix_ln_b"])),
                    (bg1[:, :], row(g.given["L0_mix_bg1"])), (wg2[0:H, :], g.given["L0_mix_Wg2"]), (wg2[H:H + 1, :], row(g.given["L0_mix_bg2"])),
                    (wp[:, :, :], by_rows(g.given["L0_mix_Wproj"])), (bp[:, :], row(g.given["L0_mix_bproj"]))])
                load_groups(sp, g, xt, loaded, used)

            @block.gpsimd
            def _(pool):
                pool.memset(hg[:, :, :, H:H + 1].rearrange("p u j o -> p (u j) o"), 1.0).then_inc(ones_set, 1)
                pool.memset(hg[:, :, :, H + 1:P].rearrange("p u j o -> p (u j) o"), 0.0).then_inc(ones_set, 1)

            @block.tensor
            def _(pe):
                pe.wait_ge(w_loaded, 16 * 8)
                pe.wait_ge(ones_set, 2)
                pe.wait_ge(prepared, 1)
                for c in range(KC):
                    pe.matmul(ps_b[:, 0:H], ln_rows[:, c, :], wg1[:, c, :], start=(c == 0), stop=False)
                pe.matmul(ps_b[:, 0:H], g.ones[0:1, :], bg1[:, :], start=False, stop=True).then_inc(bias_done, 1)

                def first_products(gi, k16, u, early):
                    pe.wait_ge(loaded[u], k16)
                    if not early:
                        pe.wait_ge(gated, gi - 1)
                    for j in range(GROUP):
                        for c in range(KC):
                            mm = pe.matmul(ps_a[u][j][:, :], chunk(xt, u, c, j), w1[:, c, :], start=(c == 0), stop=(c == KC - 1))
                    mm.then_inc(used, 1)

                def project(gi, first):
                    pe.wait_ge(kept_o, gi + 1)
                    if not first:
                        pe.wait_ge(added, gi)
                    for j in range(GROUP):
                        for c in range(KC):
                            pe.matmul(ps_e[:, j, :], pt[:, c, j * P:(j + 1) * P], wp[:, c, :], start=(c == 0), stop=False)
                        mm = pe.matmul(ps_e[:, j, :], g.ones[0:1, :], bp[:, :], start=False, stop=True)
                    mm.then_inc(out_done, 1)

                first_products(0, 16, 0, True)

                def body(k, first, last):
                    for u in range(2):
                        gi = 2 * k + u
                        start = first and u == 0
                        pe.wait_ge(bent, gi + 1)
                        if not start:
                            pe.wait_ge(kept_h, gi)
                        for j in range(GROUP):
                            mm = pe.transpose(ps_b[:, j * P:(j + 1) * P], hg[:, u, j, :], g.ident[:, :])
                        mm.then_inc(turned_h, 1)
                        if not (last and u == 1):
                            first_products(gi + 1, 16 * k + (16 if u == 0 else 32), 1 - u, start)
                        pe.wait_ge(kept_h, gi + 1)
                        if not start:
                            pe.wait_ge(gate_ready, gi)
                        for j in range(GROUP):
                            mm = pe.matmul(ps_c[:, j, :], ht[:, u, j * P:(j + 1) * P], wg2[:, :], start=True, stop=True)
                        mm.then_inc(gate_done, 1)
                        if not start:
                            project(gi - 1, first and u == 1)
                        pe.wait_ge(gated, gi + 1)
                        if not start:
                            pe.wait_ge(kept_o, gi)
                        for j in range(GROUP):
                            for c in range(KC):
                                mm = pe.transpose(ps_d[:, c, j * P:(j + 1) * P], prod[:, j, c * P:(c + 1) * P], g.ident[:, :])
                        mm.then_inc(turned_o, 1)
                peeled_both(pe, PAIRS, body)
                project(GROUPS - 1, False)

            @block.scalar
            def _(act):
                def bend(gi, u, early):
                    act.wait_ge(scaled, gi + 1)
                    if not early:
                        act.wait_ge(turned_h, gi - 1)
                    act.activation(hg[:, u, :, 0:H], hs[:, u, :, :], ACT.Gelu).then_inc(bent, 1)

                bend(0, 0, True)

                def body(k, first, last):
                    for u in range(2):
                        gi = 2 * k + u
                        act.wait_ge(turned_h, gi + 1)
                        if not first:
                            act.wait_ge(gate_done, gi - 1)
                        act.activation(ht[:, u, :], ps_b[0:H + 1, :], ACT.Copy).then_inc(kept_h, 1)
                        if not (last and u == 1):
                            bend(gi + 1, 1 - u, first and u == 0)
                        act.wait_ge(gate_done, gi + 1)
                        if not (first and u == 0):
                            act.wait_ge(gated, gi)
                        act.activation(gate[:, :, :], ps_c[:, :, :], ACT.Sigmoid).then_inc(gate_ready, 1)
                        act.wait_ge(turned_o, gi + 1)
                        if not (first and u == 0):
                            act.wait_ge(out_done, gi)
                        act.activation(pt[:, :, :], ps_d[:, :, :], ACT.Copy).then_inc(kept_o, 1)
                peeled_both(act, PAIRS, body)

            @block.vector
            def _(dve):
                dve.wait_ge(w_loaded, 16 * 8)
                for c in range(KC):
                    dve.tensor_copy(w1[:, c, 0:C], g.wqc[:, c, :])
                    dve.tensor_scalar(w1[:, c, C:C + H], wg1[:, c, :], ln_g[:, c:c + 1], None, ALU.mult)
                    op = dve.tensor_scalar(ln_rows[:, c, :], g.ones[:, :], ln_b[:, c:c + 1], None, ALU.mult)
                op.then_inc(prepared, 1)
                dve.wait_ge(bias_done, 1)
                dve.tensor_copy(h_bias[:, :], ps_b[:, 0:H]).then_inc(step, 1)
                dve.wait_ge(step, 1)

                def scale(gi, u, early):
                    dve.wait_ge(used, gi + 1)
                    if not early:
                        dve.wait_ge(bent, gi - 1)
                    for j in range(GROUP):
                        op = dve.scalar_tensor_tensor(hs[:, u, j, :], ps_a[u][j][:, C:C + H], col(g.rstd2, gi * GROUP + j),
                                                      h_bias[:, :], ALU.mult, ALU.add)
                    op.then_inc(scaled, 1)

                def add(gi):
                    dve.wait_ge(out_done, gi + 1)
                    at = g.x_sb[:, bass.ds(gi * GROUP, GROUP), :]
                    dve.tensor_tensor(at, at, ps_e[:, :, :], ALU.add).then_inc(added, 1)

                scale(0, 0, True)

                def body(k, first, last):
                    for u in range(2):
                        gi = 2 * k + u
                        if not (last and u == 1):
                            scale(gi + 1, 1 - u, first and u == 0)
                        if not (first and u == 0):
                            add(gi - 1)
                        dve.wait_ge(gate_ready, gi + 1)
                        if not (first and u == 0):
                            dve.wait_ge(turned_o, gi)
                        for j in range(GROUP):
                            op = dve.tensor_tensor(prod[:, j, :], ps_a[u][j][:, 0:C], gate[:, j, :], ALU.mult)
                        op.then_inc(gated, 1)
                peeled_both(dve, PAIRS, body)
                add(GROUPS - 1)


def expert_weights(nc, g):
    E = EXPERTS
    with phase(nc, "gates") as ph:
        loaded, iotas, step, p_in, p_out = ph.sem("loaded"), ph.sem("iotas"), ph.sem("step"), ph.sem("exp_in"), ph.sem("exp_out")
        gb = ph.sb("gb", [P, E])
        lower_i = ph.sb("lower_i", [P, E, E], I32)
        lower = ph.sb("lower", [P, E, E])
        p = ph.sb("p", [P, TILES, E])
        q = ph.sb("q", [P, TILES, E])
        top = ph.sb("top", [P, TILES])
        rank = ph.sb("rank", [P, TILES, E])
        gt = ph.sb("gt", [P, TILES, E, E])
        eq = ph.sb("eq", [P, TILES, E, E])

        def each(t):
            return t[:, :].unsqueeze(2).to_broadcast([P, TILES, E])

        with nc.Block() as block:
            @block.sync
            def _(sp):
                load_all(sp, loaded, [(gb[:, :], every(g.given["L0_ffn_gb"]))])

            @block.gpsimd
            def _(pool):
                pool.iota(lower_i[:, :, :], pattern=[[1, E], [-1, E]], base=0, channel_multiplier=0).then_inc(iotas, 1)

            @block.scalar
            def _(act):
                for k in range(2):
                    act.wait_ge(p_in, k + 1)
                    act.activation(q[:, :, :], p[:, :, :], ACT.Exp).then_inc(p_out, 1)

            @block.vector
            def _(dve):
                n = Count()

                def done(op):
                    op.then_inc(step, 1)
                    dve.wait_ge(step, n.up())

                dve.wait_ge(iotas, 1)
                done(dve.tensor_scalar(lower[:, :, :], lower_i[:, :, :], 0.0, None, ALU.is_gt))
                dve.wait_ge(loaded, 16)
                done(dve.tensor_tensor(p[:, :, :], g.logits[:, :, :], gb[:, :].unsqueeze(1).to_broadcast([P, TILES, E]), ALU.add))
                done(dve.tensor_reduce(top[:, :], p[:, :, :], AX, ALU.max))
                dve.tensor_tensor(p[:, :, :], p[:, :, :], each(top), ALU.subtract).then_inc(p_in, 1)
                dve.wait_ge(p_out, 1)
                done(dve.tensor_reduce(top[:, :], q[:, :, :], AX, ALU.add))
                done(dve.reciprocal(top[:, :], top[:, :]))
                done(dve.tensor_tensor(p[:, :, :], q[:, :, :], each(top), ALU.mult))
                pe_ = p[:, :, :].unsqueeze(3).to_broadcast([P, TILES, E, E])
                pj_ = p[:, :, :].unsqueeze(2).to_broadcast([P, TILES, E, E])
                for e in range(E):
                    dve.tensor_tensor(gt[:, :, e, :], p[:, :, :], pe_[:, :, e, :], ALU.is_gt)
                    done(dve.tensor_tensor(eq[:, :, e, :], p[:, :, :], pe_[:, :, e, :], ALU.is_equal))
                    done(dve.tensor_tensor(eq[:, :, e, :], eq[:, :, e, :], lower[:, e, :].unsqueeze(1).to_broadcast([P, TILES, E]), ALU.mult))
                done(dve.tensor_tensor(gt[:, :, :, :], gt[:, :, :, :], eq[:, :, :, :], ALU.add))
                done(dve.tensor_reduce(rank[:, :, :], gt[:, :, :, :], AX, ALU.add))
                done(dve.tensor_scalar(rank[:, :, :], rank[:, :, :], 2.0, None, ALU.is_lt))
                done(dve.tensor_reduce(top[:, :], p[:, :, :], AX, ALU.max))
                dve.tensor_tensor(p[:, :, :], p[:, :, :], each(top), ALU.subtract).then_inc(p_in, 1)
                dve.wait_ge(p_out, 2)
                done(dve.tensor_tensor(q[:, :, :], q[:, :, :], rank[:, :, :], ALU.mult))
                done(dve.tensor_reduce(top[:, :], q[:, :, :], AX, ALU.add))
                done(dve.reciprocal(top[:, :], top[:, :]))
                dve.tensor_tensor(g.mix5[:, :, 0:E], q[:, :, :], each(top), ALU.mult)
                dve.memset(g.mix5[:, :, E:E + 1], 1.0)


def ffn0(nc, g):
    E = EXPERTS
    with phase(nc, "ffn0") as ph:
        loaded, used = [ph.sem("loaded0"), ph.sem("loaded1")], ph.sem("used")
        w_loaded, h1_act, h1_dve, second_done, turned_w, kept_w, h2_act, h2_dve, weighed, out_done, added = (
            ph.sem(s) for s in ("w_loaded", "h1_act", "h1_dve", "second_done", "turned_w", "kept_w", "h2_act", "h2_dve",
                                "weighed", "out_done", "added"))
        xt = ph.sb("xt", [P, 2, KC * ROWS])
        sw1 = ph.sb("sw1", [P, KC, C])
        ew1 = ph.sb("ew1", [P, KC, E, P])
        sw2 = ph.sb("sw2", [P, 2, P])
        ew2 = ph.sb("ew2", [P, E, 64])
        sw3 = ph.sb("sw3", [P, C])
        ew3 = ph.sb("ew3", [P, 2, C])
        b3 = ph.sb("b3", [E + 1, C])
        sb1 = ph.sb("sb1", [P, 2])
        eb1 = ph.sb("eb1", [P, E])
        sb2 = ph.sb("sb2", [P, 1])
        eb2 = ph.sb("eb2", [P, 2])
        h1 = ph.sb("h1", [P, 2 + E, ROWS])
        hs2 = ph.sb("hs2", [P, ROWS])
        he2 = ph.sb("he2", [P, 2, ROWS])
        hw2 = ph.sb("hw2", [P, 2, ROWS])
        wt = ph.sb("wt", [E + 1, ROWS])
        w5 = ph.sb("w5", [P, GROUP, E + 1])
        staged_w = ph.sem("staged_w")
        ps_h = [ph.psum(f"h{i}", [P, 2, ROWS]) for i in range(3)]
        ps_e = ph.psum("e", [P, 2, ROWS])
        ps_s = ph.psum("s", [P, ROWS])
        ps_t = ph.psum("t", [P, ROWS])
        ps_w = ph.psum("w", [P, 2, ROWS])
        ps_o = ph.psum("o", [P, GROUP, C])
        with nc.Block() as block:
            @block.sync
            def _(sp):
                load_all(sp, w_loaded, [
                    (sw1[:, :, :], by_rows(g.given["L0_ffn_sW1"])),
                    (ew1[:, 0, :, :], g.given["L0_ffn_eW1"][:, 0:P, :].rearrange("e p n -> p e n")),
                    (ew1[:, 1, :, :], g.given["L0_ffn_eW1"][:, P:C, :].rearrange("e p n -> p e n")),
                    (sw2[:, :, :], by_rows(g.given["L0_ffn_sW2"])), (ew2[:, :, :], g.given["L0_ffn_eW2"].rearrange("e p n -> p e n")),
                    (sw3[:, :], g.given["L0_ffn_sW3"]), (ew3[:, :, :], by_rows(g.given["L0_ffn_eW3"].rearrange("e p n -> (e p) n"))),
                    (b3[0:E, :], g.given["L0_ffn_eb3"]), (b3[E:E + 1, :], row(g.given["L0_ffn_sb3"])),
                    (sb1[:, :], columns(g.given["L0_ffn_sb1"])), (sb2[:, :], columns(g.given["L0_ffn_sb2"])),
                    (eb1[:, :], g.given["L0_ffn_eb1"].rearrange("e p -> p e")), (eb2[:, :], columns(g.given["L0_ffn_eb2"].rearrange("e p -> (e p)")))])
                load_groups(sp, g, xt, loaded, used)

            @block.tensor
            def _(pe):
                pe.wait_ge(w_loaded, 16 * 13)

                def last_products(gi, first):
                    pe.wait_ge(h2_dve, gi + 1)
                    pe.wait_ge(weighed, gi + 1)
                    if not first:
                        pe.wait_ge(added, gi)
                    for j in range(GROUP):
                        at = slice(j * P, (j + 1) * P)
                        pe.matmul(ps_o[:, j, :], hs2[:, at], sw3[:, :], start=True, stop=False)
                        for q in range(2):
                            pe.matmul(ps_o[:, j, :], hw2[:, q, at], ew3[:, q, :], start=False, stop=False)
                        mm = pe.matmul(ps_o[:, j, :], wt[:, at], b3[:, :], start=False, stop=True)
                    mm.then_inc(out_done, 1)

                def body(k, first):
                    for u in range(2):
                        gi = 2 * k + u
                        start = first and u == 0
                        pe.wait_ge(loaded[u], 16 * k + 16)
                        if not start:
                            pe.wait_ge(h1_act, gi)
                            pe.wait_ge(h1_dve, gi)
                        for m in range(2 + E):
                            for c in range(KC):
                                w = sw1[:, c, m * P:(m + 1) * P] if m < 2 else ew1[:, c, m - 2, :]
                                mm = pe.matmul(ps_h[m // 2][:, m % 2, :], w, chunk(xt, u, c), start=(c == 0), stop=(c == KC - 1))
                        mm.then_inc(used, 1)
                        if not start:
                            last_products(gi - 1, first and u == 1)
                        pe.wait_ge(staged_w, gi + 1)
                        for j in range(GROUP):
                            mm = pe.transpose(ps_t[0:E + 1, j * P:(j + 1) * P], w5[:, j, :], g.ident[:, :])
                        mm.then_inc(turned_w, 1)
                        pe.wait_ge(h1_act, gi + 1)
                        pe.wait_ge(h1_dve, gi + 1)
                        for c in range(2):
                            pe.matmul(ps_s[:, :], sw2[:, c, :], h1[:, c, :], start=(c == 0), stop=(c == 1))
                        for e in range(E):
                            at = slice((e % 2) * 64, (e % 2) * 64 + 64)
                            pe.matmul(ps_e[at, e // 2, :], ew2[:, e, :], h1[:, 2 + e, :], start=True, stop=True)
                        pe.wait_ge(kept_w, gi + 1)
                        for q in range(2):
                            mm = pe.matmul(ps_w[:, q, :], g.half[0:E, q, :], wt[0:E, :], start=True, stop=True)
                        mm.then_inc(second_done, 1)
                peeled(pe, PAIRS, body)
                last_products(GROUPS - 1, False)

            @block.scalar
            def _(act):
                act.wait_ge(w_loaded, 16 * 13)

                def body(k, first):
                    for u in range(2):
                        gi = 2 * k + u
                        start = first and u == 0
                        act.wait_ge(used, gi + 1)
                        if not start:
                            act.wait_ge(second_done, gi)
                        for m in (0, 1, 4, 5):
                            bias = sb1[:, m:m + 1] if m < 2 else eb1[:, m - 2:m - 1]
                            op = act.activation(h1[:, m, :], ps_h[m // 2][:, m % 2, :], ACT.Relu, bias=bias)
                        op.then_inc(h1_act, 1)
                        act.wait_ge(turned_w, gi + 1)
                        if not start:
                            act.wait_ge(out_done, gi)
                        act.activation(wt[:, :], ps_t[0:E + 1, :], ACT.Copy).then_inc(kept_w, 1)
                        act.wait_ge(second_done, gi + 1)
                        if not start:
                            act.wait_ge(weighed, gi)
                        for q in range(2):
                            op = act.activation(he2[:, q, :], ps_e[:, q, :], ACT.Relu, bias=eb2[:, q:q + 1])
                        op.then_inc(h2_act, 1)
                peeled(act, PAIRS, body)

            @block.vector
            def _(dve):
                dve.wait_ge(w_loaded, 16 * 13)

                def add(gi):
                    dve.wait_ge(out_done, gi + 1)
                    at = g.x_sb[:, bass.ds(gi * GROUP, GROUP), :]
                    dve.tensor_tensor(at, at, ps_o[:, :, :], ALU.add).then_inc(added, 1)

                def body(k, first):
                    for u in range(2):
                        gi = 2 * k + u
                        start = first and u == 0
                        if not start:
                            dve.wait_ge(turned_w, gi)
                        dve.tensor_copy(w5[:, :, :], g.mix5[:, bass.ds(gi * GROUP, GROUP), :]).then_inc(staged_w, 1)
                        dve.wait_ge(used, gi + 1)
                        if not start:
                            dve.wait_ge(second_done, gi)
                        for m in (2, 3):
                            op = dve.tensor_scalar(h1[:, m, :], ps_h[m // 2][:, m % 2, :], eb1[:, m - 2:m - 1], 0.0, ALU.add, ALU.max)
                        op.then_inc(h1_dve, 1)
                        if not start:
                            add(gi - 1)
                        dve.wait_ge(second_done, gi + 1)
                        dve.tensor_scalar(hs2[:, :], ps_s[:, :], sb2[:, 0:1], 0.0, ALU.add, ALU.max).then_inc(h2_dve, 1)
                        dve.wait_ge(h2_act, gi + 1)
                        dve.tensor_tensor(hw2[:, :, :], he2[:, :, :], ps_w[:, :, :], ALU.mult).then_inc(weighed, 1)
                peeled(dve, PAIRS, body)
                add(GROUPS - 1)


def node_tables(nc, g):
    H, D = GAT_HEADS, GAT_D
    with phase(nc, "tab") as ph:
        loaded, used = [ph.sem("loaded0"), ph.sem("loaded1")], ph.sem("used")
        w_loaded, step, root_in, root_out, w_ready = (ph.sem(s) for s in ("w_loaded", "step", "root_in", "root_out", "w_ready"))
        act_done, dve_done, terms_stored = ph.sem("act_done"), ph.sem("dve_done"), ph.sem("terms_stored")
        stored = [ph.sem("stored0"), ph.sem("stored1")]
        xt = ph.sb("xt", [P, 2, KC * ROWS])
        wgcn = ph.sb("wgcn", [P, KC, C])
        wgat = ph.sb("wgat", [P, KC, C + 2 * H])
        a = ph.sb("a", [P, 2, C])
        wa = ph.sb("wa", [P, C])
        deg = ph.sb("deg", [P, TILES])
        root = ph.sb("root", [P, TILES])
        rows = ph.sb("rows", [P, 2, GROUP, 2 * C])
        ps_g = [[ph.psum(f"g{u}{j}", [P, C]) for j in range(GROUP)] for u in range(2)]
        ps_a = [[ph.psum(f"a{u}{j}", [P, C + 2 * H]) for j in range(GROUP)] for u in range(2)]
        with nc.Block() as block:
            @block.sync
            def _(sp):
                load_all(sp, w_loaded, [
                    (wgcn[:, :, :], by_rows(g.given["L1_gnn_W_gcn"])), (wgat[:, :, 0:C], by_rows(g.given["L1_gnn_W_gat"])),
                    (a[:, 0, :], every(g.given["L1_gnn_a_src"].rearrange("h d -> (h d)"))),
                    (a[:, 1, :], every(g.given["L1_gnn_a_dst"].rearrange("h d -> (h d)")))])
                load_groups(sp, g, xt, loaded, used)
                sp.wait_ge(dve_done, GROUPS)
                with nc.allow_non_contiguous_dma(reason="four words of each node"):
                    sp.dma_start(g.src_terms.rearrange("(t p) h -> p t h", p=P), g.terms[:, :, 0:H]).then_inc(terms_stored, 16)
                sp.wait_ge(terms_stored, 16)

            @block.gpsimd
            def _(pool):
                def body(k, first):
                    for u in range(2):
                        pool.wait_ge(act_done, 2 * k + u + 1)
                        pool.wait_ge(dve_done, 2 * k + u + 1)
                        pool.dma_start(g.node_rows[bass.ds((2 * k + u) * ROWS, ROWS), :].rearrange("(j p) c -> p j c", p=P),
                                       rows[:, u, :, :]).then_inc(stored[u], 16)
                peeled(pool, PAIRS, body)
                for u in range(2):
                    pool.wait_ge(stored[u], 16 * PAIRS)

            @block.tensor
            def _(pe):
                pe.wait_ge(w_ready, 1)

                def body(k, first):
                    for u in range(2):
                        pe.wait_ge(loaded[u], 16 * k + 16)
                        if not first:
                            pe.wait_ge(act_done, 2 * k + u - 1)
                            pe.wait_ge(dve_done, 2 * k + u - 1)
                        for j in range(GROUP):
                            for c in range(KC):
                                pe.matmul(ps_g[u][j][:, :], chunk(xt, u, c, j), wgcn[:, c, :], start=(c == 0), stop=(c == KC - 1))
                            for c in range(KC):
                                mm = pe.matmul(ps_a[u][j][:, :], chunk(xt, u, c, j), wgat[:, c, :], start=(c == 0), stop=(c == KC - 1))
                        mm.then_inc(used, 1)
                peeled(pe, PAIRS, body)

            @block.scalar
            def _(act):
                act.wait_ge(root_in, 1)
                act.activation(root[:, :], deg[:, :], ACT.Sqrt).then_inc(root_out, 1)
                act.wait_ge(w_ready, 1)

                def body(k, first):
                    for u in range(2):
                        gi = 2 * k + u
                        act.wait_ge(used, gi + 1)
                        if not first:
                            act.wait_ge(stored[u], 16 * k)
                        for j in range(GROUP):
                            op = act.activation(rows[:, u, j, 0:C], ps_g[u][j][:, :], ACT.Copy, scale=col(g.dinv, gi * GROUP + j))
                        op.then_inc(act_done, 1)
                peeled(act, PAIRS, body)

            @block.vector
            def _(dve):
                n = Count()

                def done(op):
                    op.then_inc(step, 1)
                    dve.wait_ge(step, n.up())

                dve.wait_ge(w_loaded, 64)
                for c in range(KC):
                    for s in range(2):
                        done(dve.tensor_tensor(wa[:, :], wgat[:, c, 0:C], a[:, s, :], ALU.mult))
                        done(dve.tensor_reduce(wgat[:, c, C + s * H:C + s * H + H], wa[:, :].rearrange("p (h d) -> p h d", h=H), AX, ALU.add))
                done(dve.memset(g.dinv[:, :], 0.0))
                done(dve.memset(deg[:, :], 1.0))
                done(dve.tensor_scalar(g.dinv[:, 0:NODE_BLOCKS], g.deg_cnt[:, :, 0], 1.0, None, ALU.add))
                done(dve.tensor_scalar(deg[:, 0:NODE_BLOCKS], g.dinv[:, 0:NODE_BLOCKS], 1e-12, None, ALU.max))
                dve.tensor_scalar(g.dinv[:, :], g.dinv[:, :], 0.0, None, ALU.is_gt).then_inc(root_in, 1)
                dve.wait_ge(root_out, 1)
                done(dve.reciprocal(root[:, :], root[:, :]))
                dve.tensor_tensor(g.dinv[:, :], g.dinv[:, :], root[:, :], ALU.mult).then_inc(w_ready, 1)

                def body(k, first):
                    for u in range(2):
                        gi = 2 * k + u
                        dve.wait_ge(used, gi + 1)
                        if not first:
                            dve.wait_ge(stored[u], 16 * k)
                        for j in range(GROUP):
                            dve.tensor_copy(rows[:, u, j, C:2 * C], ps_a[u][j][:, 0:C])
                            op = dve.tensor_copy(g.terms[:, bass.ds(gi * GROUP + j, 1), :].rearrange("p o c -> p (o c)"), ps_a[u][j][:, C:C + 2 * H])
                        op.then_inc(dve_done, 1)
                peeled(dve, PAIRS, body)


def edge_ranges(nc, g):
    N = NODE_BLOCKS
    with phase(nc, "ranges") as ph:
        counts_ready, summed, step = ph.sem("counts_ready"), ph.sem("summed"), ph.sem("step")
        cnt = ph.sb("cnt", [P, N])
        tot = ph.sb("tot", [P, N])
        run = ph.sb("run", [P, N])
        first = ph.sb("first", [P, N])
        none = ph.sb("none", [P, N])
        ps_in = ph.psum("in", [P, N])
        ps_tot = ph.psum("tot", [P, N])
        with nc.Block() as block:
            @block.vector
            def _(dve):
                n = Count()

                def done(op):
                    op.then_inc(step, 1)
                    dve.wait_ge(step, n.up())

                dve.tensor_copy(cnt[:, :], g.deg_cnt[:, :, 1]).then_inc(counts_ready, 1)
                dve.wait_ge(summed, 1)
                done(dve.tensor_copy(tot[:, :], ps_tot[:, :]))
                done(dve.tensor_tensor_scan(run[:, :], g.ones[:, 0:N], tot[:, :], 0.0, ALU.mult, ALU.add))
                done(dve.tensor_tensor(run[:, :], run[:, :], tot[:, :], ALU.subtract))
                done(dve.tensor_tensor(first[:, :], run[:, :], ps_in[:, :], ALU.add))
                done(dve.tensor_scalar(none[:, :], cnt[:, :], 0.0, None, ALU.is_equal))
                dve.scalar_tensor_tensor(g.first_edge[:, :], none[:, :], float(FAR), first[:, :], ALU.mult, ALU.add)
                dve.tensor_scalar(g.no_edge[:, :], none[:, :], -BIG, None, ALU.mult)
                done(dve.tensor_tensor(first[:, :], first[:, :], cnt[:, :], ALU.add))
                dve.tensor_scalar(g.last_edge[:, :], first[:, :], -1.0, 0.0, ALU.add, ALU.max)

            @block.tensor
            def _(pe):
                pe.wait_ge(counts_ready, 1)
                pe.matmul(ps_in[:, :], g.upper[:, :], cnt[:, :], start=True, stop=True)
                pe.matmul(ps_tot[:, :], g.ones[:, :], cnt[:, :], start=True, stop=True).then_inc(summed, 1)


SPAN = 7
assert NODE_BLOCKS % SPAN == 0


def attention(nc, g):
    H = GAT_HEADS
    with phase(nc, "att") as ph:
        dst_loaded, terms_loaded = ph.sem("dst_loaded"), ph.sem("terms_loaded")
        vals_ready, span_staged, scattered, table_loaded = (ph.sem(s) for s in ("vals_ready", "span_staged", "scattered", "table_loaded"))
        step, asked, turned, back = (ph.sem(s) for s in ("step", "asked", "turned", "back"))
        runs_ready, runs_stored, tops_landed, tops_ready, tops_kept = (
            ph.sem(s) for s in ("runs_ready", "runs_stored", "tops_landed", "tops_ready", "tops_kept"))
        e_ready, e_done, e_stored = (ph.sem(s) for s in ("e_ready", "e_done", "e_stored"))
        terms = ph.sb("edge_terms", [P, PER, H])
        same = ph.sb("same", [P, PER], BF16)
        cut = ph.sb("cut", [P, PER], BF16)
        lead = ph.sb("lead", [P, PER], BF16)
        led = ph.sb("led", [P, PER], BF16)
        stage_i = ph.sb("stage_i", [P, SPAN], U32)
        stage_v = ph.sb("stage_v", [P, SPAN, H])
        full = ph.sb("full", [P, H])
        ends = ph.sb("ends", [P, H])
        ft = ph.sb("ft", [H, P])
        ct = ph.sb("ct", [H, P])
        et = ph.sb("et", [H, P])
        it = ph.sb("it", [H, P])
        init = ph.sb("init", [P, H])
        self_e = ph.sb("self_e", [P, NODE_BLOCKS, H])
        ps_t = ph.psum("t", [P, 4, P])
        flat_dst = g.dstP.rearrange("t p -> (t p)")
        M = NODE_BLOCKS // SPAN

        def part_major(table):
            return table[0:PAD_EDGES, :].rearrange("(q j) h -> q (j h)", q=P)

        with ExitStack() as early:
            dst2 = early.enter_context(nc.sbuf_tensor("att_dst2", [P, PER + 1], I32))
            with nc.Block() as block:
                @block.sync
                def _(sp):
                    sp.dma_start(dst2[:, 1:PER + 1], flat_dst.rearrange("(q j) -> q j", q=P)).then_inc(dst_loaded, 16)
                    with nc.allow_non_contiguous_dma(reason="last edge of each row above"):
                        sp.dma_start(dst2[1:P, 0:1], flat_dst[0:(P - 1) * PER].rearrange("(q j) -> q j", j=PER)[:, PER - 1:PER]).then_inc(dst_loaded, 16)

                @block.vector
                def _(dve):
                    n = Count()

                    def done(op):
                        op.then_inc(step, 1)
                        dve.wait_ge(step, n.up())

                    dve.memset(dst2[0:1, 0:1], -1)
                    done(dve.memset(full[:, :], 0.0))
                    dve.wait_ge(dst_loaded, 32)
                    done(dve.tensor_tensor(same[:, :], dst2[:, 1:PER + 1], dst2[:, 0:PER], ALU.is_equal))
                    done(dve.tensor_scalar(cut[:, :], same[:, :], 1.0, BIG, ALU.subtract, ALU.mult))
                    done(dve.tensor_tensor_scan(lead[:, :], cut[:, :], cut[:, :], 0.0, ALU.add, ALU.min))
                    done(dve.tensor_scalar(led[:, :], lead[:, :], 0.0, None, ALU.is_ge))
                    dve.tensor_reduce(full[:, 0:1], same[:, :], AX, ALU.min)
                    done(dve.tensor_tensor(self_e[:, :, :], g.terms[:, 0:NODE_BLOCKS, 0:H], g.terms[:, 0:NODE_BLOCKS, H:2 * H], ALU.add))
                    done(dve.scalar_tensor_tensor(self_e[:, :, :], self_e[:, :, :], 0.2, self_e[:, :, :], ALU.mult, ALU.max))

        issued = ph.sem("issued")
        val = ph.sb("val", [P, PER, H])
        base = 7
        with nc.Block() as block:
            @block.gpsimd
            def _(pool):
                def scatter(table, turn):
                    def span(k, first):
                        if not (first and turn == 0):
                            pool.wait_ge(scattered, 16 * SPAN * (turn * M + k))
                        pool.tensor_copy(stage_i[:, :], g.first_edge[:, bass.ds(k * SPAN, SPAN)])
                        pool.tensor_copy(stage_v[:, :, :], g.node_vals[:, bass.ds(k * SPAN, SPAN), :]).then_inc(span_staged, 1)
                        pool.wait_ge(span_staged, turn * M + k + 1)
                        pool.sem_inc(issued, 1)
                        pool.wait_ge(vals_ready, 1)
                        for i in range(SPAN):
                            pool.indirect_dma_start(table, bass.IndirectOffsetOnAxis(stage_i[:, i:i + 1], 0), stage_v[:, i, :], None,
                                                    bounds_check=PAD_EDGES - 1, oob_is_err=False).then_inc(scattered, 16)
                    peeled(pool, M, span)
                    pool.wait_ge(scattered, 16 * SPAN * (turn + 1) * M)

                pool.wait_ge(vals_ready, 1)
                scatter(g.dst_terms, 0)
                pool.wait_ge(runs_stored, 16)

                def fetch(k, first):
                    if not first:
                        pool.wait_ge(tops_kept, k)
                    pool.tensor_copy(stage_i[:, :], g.last_edge[:, bass.ds(k * SPAN, SPAN)]).then_inc(span_staged, 1)
                    pool.wait_ge(span_staged, M + k + 1)
                    pool.sem_inc(issued, 1)
                    pool.wait_ge(vals_ready, 1)
                    for i in range(SPAN):
                        pool.indirect_dma_start(stage_v[:, i, :], None, g.runs,
                                                bass.IndirectOffsetOnAxis(stage_i[:, i:i + 1], 0)).then_inc(tops_landed, 16)
                    pool.wait_ge(tops_landed, 16 * SPAN * (k + 1))
                    pool.tensor_copy(g.node_vals[:, bass.ds(k * SPAN, SPAN), :], stage_v[:, :, :]).then_inc(tops_kept, 1)
                peeled(pool, M, fetch)
                pool.wait_ge(tops_ready, 1)

                def spread(k, first):
                    if not first:
                        pool.wait_ge(scattered, 16 * SPAN * (M + k))
                    pool.tensor_copy(stage_i[:, :], g.first_edge[:, bass.ds(k * SPAN, SPAN)])
                    pool.tensor_copy(stage_v[:, :, :], g.node_vals[:, bass.ds(k * SPAN, SPAN), :]).then_inc(span_staged, 1)
                    pool.wait_ge(span_staged, 2 * M + k + 1)
                    pool.sem_inc(issued, 1)
                    pool.wait_ge(vals_ready, 1)
                    for i in range(SPAN):
                        pool.indirect_dma_start(g.max_terms, bass.IndirectOffsetOnAxis(stage_i[:, i:i + 1], 0), stage_v[:, i, :], None,
                                                bounds_check=PAD_EDGES - 1, oob_is_err=False).then_inc(scattered, 16)
                peeled(pool, M, spread)
                pool.wait_ge(scattered, 16 * SPAN * 2 * M)

            @block.sync
            def _(sp):
                sp.dma_start(terms[:, :, :].rearrange("p j h -> p (j h)"), g.edge_terms).then_inc(terms_loaded, 16)
                sp.wait_ge(scattered, 16 * SPAN * M)
                sp.dma_start(val[:, 0:PER, :].rearrange("p j h -> p (j h)"), part_major(g.dst_terms)).then_inc(table_loaded, 16)
                sp.wait_ge(runs_ready, 1)
                sp.dma_start(part_major(g.runs), val[:, 0:PER, :].rearrange("p j h -> p (j h)")).then_inc(runs_stored, 16)
                sp.wait_ge(scattered, 16 * SPAN * 2 * M)
                sp.dma_start(val[:, 0:PER, :].rearrange("p j h -> p (j h)"), part_major(g.max_terms)).then_inc(table_loaded, 16)
                sp.wait_ge(e_done, 1)
                sp.dma_start(g.ee_rows.rearrange("t c -> (t c)").rearrange("(q n) -> q n", q=P),
                             terms[:, 0:PER, :].rearrange("p j h -> p (j h)")).then_inc(e_stored, 16)
                sp.wait_ge(e_stored, 16)

            @block.tensor
            def _(pe):
                for k in range(3):
                    pe.wait_ge(asked, k + 1)
                    pe.transpose(ps_t[0:H, 0, :], full[:, :], g.ident[:, :])
                    pe.transpose(ps_t[0:H, 1, :], ends[:, :], g.ident[:, :]).then_inc(turned, 1)
                    pe.wait_ge(back, k + 1)
                    pe.transpose(ps_t[:, 2, 0:H], it[:, :], g.ident[0:H, 0:H]).then_inc(turned, 1)

            @block.scalar
            def _(act):
                act.wait_ge(e_ready, 1)
                act.activation(terms[:, 0:PER, :].rearrange("p j h -> p (j h)"), terms[:, 0:PER, :].rearrange("p j h -> p (j h)"),
                               ACT.Exp).then_inc(e_done, 1)
                act.wait_ge(tops_ready, 1)
                act.activation(g.self_ee[:, :, :], self_e[:, :, :], ACT.Exp).then_inc(e_done, 1)

            @block.vector
            def _(dve):
                n = Count(base)

                def done(op):
                    op.then_inc(step, 1)
                    dve.wait_ge(step, n.up())

                dve.tensor_copy(g.node_vals[:, :, :], g.terms[:, 0:NODE_BLOCKS, H:2 * H]).then_inc(vals_ready, 1)
                done(dve.tensor_copy(full[:, 1:H], full[:, 0:1].to_broadcast([P, H - 1])))

                def carry(k, low, op0, op1, pen):
                    done(dve.tensor_copy(ends[:, :], val[:, PER - 1, :]))
                    dve.sem_inc(asked, 1)
                    dve.wait_ge(turned, 2 * k + 1)
                    if pen:
                        done(dve.tensor_scalar(ft[:, :], ps_t[0:H, 0, :], 1.0, BIG, ALU.subtract, ALU.mult))
                    else:
                        done(dve.tensor_copy(ft[:, :], ps_t[0:H, 0, :]))
                    done(dve.tensor_copy(et[:, :], ps_t[0:H, 1, :]))
                    done(dve.tensor_tensor_scan(ct[:, :], ft[:, :], et[:, :], low, op0, op1))
                    dve.memset(it[:, 0:1], low)
                    done(dve.tensor_copy(it[:, 1:P], ct[:, 0:P - 1]))
                    dve.sem_inc(back, 1)
                    dve.wait_ge(turned, 2 * k + 2)
                    done(dve.tensor_copy(init[:, :], ps_t[:, 2, 0:H]))

                def fill(k):
                    for h in range(H):
                        op = dve.tensor_tensor_scan(val[:, 0:PER, h], same[:, :], val[:, 0:PER, h], 0.0, ALU.mult, ALU.add)
                    done(op)
                    carry(k, 0.0, ALU.mult, ALU.add, False)
                    for h in range(H):
                        op = dve.scalar_tensor_tensor(val[:, 0:PER, h], led[:, :], init[:, h:h + 1], val[:, 0:PER, h], ALU.mult, ALU.add)
                    done(op)

                dve.wait_ge(table_loaded, 16)
                fill(0)
                dve.wait_ge(terms_loaded, 16)
                e = terms[:, 0:PER, :].rearrange("p j h -> p (j h)")
                v = val[:, 0:PER, :].rearrange("p j h -> p (j h)")
                done(dve.tensor_tensor(e, e, v, ALU.add))
                done(dve.scalar_tensor_tensor(e, e, 0.2, e, ALU.mult, ALU.max))
                for h in range(H):
                    op = dve.tensor_tensor_scan(val[:, 0:PER, h], cut[:, :], terms[:, 0:PER, h], -BIG, ALU.add, ALU.max)
                done(op)
                carry(1, -BIG, ALU.add, ALU.max, True)
                for h in range(H):
                    op = dve.scalar_tensor_tensor(val[:, 0:PER, h], lead[:, :], init[:, h:h + 1], val[:, 0:PER, h], ALU.add, ALU.max)
                op.then_inc(runs_ready, 1)
                dve.wait_ge(tops_kept, M)
                done(dve.tensor_tensor(g.node_vals[:, :, :], g.node_vals[:, :, :],
                                       g.no_edge[:, :].unsqueeze(2).to_broadcast([P, NODE_BLOCKS, H]), ALU.add))
                done(dve.tensor_tensor(g.node_vals[:, :, :], g.node_vals[:, :, :], self_e[:, :, :], ALU.max))
                dve.tensor_tensor(self_e[:, :, :], self_e[:, :, :], g.node_vals[:, :, :], ALU.subtract).then_inc(tops_ready, 1)
                dve.wait_ge(table_loaded, 32)
                fill(2)
                done(dve.tensor_tensor(e, e, v, ALU.subtract))
                dve.tensor_scalar(e, e, 0.0, None, ALU.min).then_inc(e_ready, 1)
                dve.wait_ge(e_done, 2)


def edge_items(nc, g):
    H = GAT_HEADS
    with phase(nc, "eei") as ph:
        landed, item_turned, item_kept = [ph.sem("landed0"), ph.sem("landed1")], ph.sem("item_turned"), ph.sem("item_kept")
        rows = [ph.sb(f"rows{u}", [P, P * H]) for u in range(2)]
        ps = ph.psum("i", [P, 2, 512])
        with nc.Block() as block:
            @block.gpsimd
            def _(pool):
                for k in range(ITEM_GROUPS):
                    if k >= 2:
                        pool.wait_ge(item_turned, k - 1)
                    pool.indirect_dma_start(rows[k % 2][:, :], None, g.ee_rows,
                                            bass.IndirectOffsetOnAxis(g.tile_of[:, k:k + 1], 0)).then_inc(landed[k % 2], 16)

            @block.tensor
            def _(pe):
                for k in range(ITEM_GROUPS):
                    pe.wait_ge(landed[k % 2], 16 * (k // 2 + 1))
                    if k >= 2:
                        pe.wait_ge(item_kept, k - 1)
                    for h in range(H):
                        mm = pe.transpose(ps[:, k % 2, h * P:(h + 1) * P],
                                          rows[k % 2][:, :].rearrange("p (e h) -> p h e", h=H)[:, h, :], g.ident[:, :])
                    mm.then_inc(item_turned, 1)

            @block.vector
            def _(dve):
                for k in range(ITEM_GROUPS):
                    dve.wait_ge(item_turned, k + 1)
                    dve.tensor_copy(g.ee_item[:, k * P:(k + 1) * P, :], ps[:, k % 2, :].rearrange("p (h e) -> p e h", h=H)).then_inc(item_kept, 1)


def own_rows(nc, g):
    H = GAT_HEADS
    with phase(nc, "own") as ph:
        loaded, stored = [ph.sem("loaded0"), ph.sem("loaded1")], [ph.sem("stored0"), ph.sem("stored1")]
        done = ph.sem("done")
        rows = ph.sb("rows", [P, 2, GROUP, C])
        outr = ph.sb("outr", [P, 2, GROUP, C + H])
        PB = NODE_BLOCKS // GROUP
        with nc.Block() as block:
            @block.sync
            def _(sp):
                for gi in range(2):
                    sp.dma_start(rows[:, gi, :, :], g.node_rows[gi * ROWS:(gi + 1) * ROWS, C:2 * C].rearrange("(j p) c -> p j c", p=P)).then_inc(loaded[gi], 16)
                with sp.Fori(1, PB // 2) as k:
                    for u in range(2):
                        sp.wait_ge(done, 2 * k + u - 1)
                        sp.dma_start(rows[:, u, :, :], g.node_rows[bass.ds((2 * k + u) * ROWS, ROWS), C:2 * C].rearrange("(j p) c -> p j c", p=P)).then_inc(loaded[u], 16)
                sp.wait_ge(done, PB - 2)
                sp.dma_start(rows[:, 0, :, :], g.node_rows[(PB - 1) * ROWS:PB * ROWS, C:2 * C].rearrange("(j p) c -> p j c", p=P)).then_inc(loaded[0], 16)

            @block.vector
            def _(dve):
                def one(gi, u, count, first):
                    dve.wait_ge(loaded[u], 16 * count)
                    if not first:
                        dve.wait_ge(stored[u], 16 * (count - 1))
                    for j in range(GROUP):
                        ee = g.self_ee[:, bass.ds(gi * GROUP + j, 1), :].rearrange("p o h -> p (o h)")
                        dve.tensor_tensor(outr[:, u, j, 0:C].rearrange("p (h d) -> p h d", h=H), rows[:, u, j, :].rearrange("p (h d) -> p h d", h=H),
                                          ee.unsqueeze(2).to_broadcast([P, H, GAT_D]), ALU.mult)
                        op = dve.tensor_copy(outr[:, u, j, C:C + H], ee)
                    op.then_inc(done, 1)

                def body(k, first):
                    for u in range(2):
                        one(2 * k + u, u, k + 1, first)
                peeled(dve, PB // 2, body)
                one(PB - 1, 0, PB // 2 + 1, False)

            @block.scalar
            def _(act):
                def one(gi, u):
                    act.wait_ge(done, gi + 1)
                    act.dma_start(g.own[bass.ds(gi * ROWS, ROWS), :].rearrange("(j p) c -> p j c", p=P), outr[:, u, :, :]).then_inc(stored[u], 16)

                def body(k, first):
                    for u in range(2):
                        one(2 * k + u, u)
                peeled(act, PB // 2, body)
                one(PB - 1, 0)
                act.wait_ge(stored[0], 16 * (PB // 2 + 1))
                act.wait_ge(stored[1], 16 * (PB // 2))


def aggregate1(nc, g):
    H = GAT_HEADS
    BANK = 512
    with phase(nc, "agg1") as ph:
        staged, landed = ph.sem("staged"), [ph.sem(f"landed{u}") for u in range(RING)]
        issued = ph.sem("issued")
        sel_ready, item_used = ph.sem("sel_ready"), ph.sem("item_used")
        own_loaded = [ph.sem("own_loaded0"), ph.sem("own_loaded1")]
        opened, sum_ready, sum_kept = ph.sem("opened"), ph.sem("sum_ready"), ph.sem("sum_kept")
        sum_stored = [ph.sem("sum_stored0"), ph.sem("sum_stored1")]
        own_relay, begun = ph.sem("own_relay"), ph.sem("begun")
        RW = 2 * C
        AW = C + H
        stage = ph.sb("stage", [P, RING], U32)
        rows = ph.sb("rows", [P, RING, RW])
        att = ph.sb("att", [P, RING, AW])
        sel_w = ph.sb("sel_w", [P, RING, P])
        sel = ph.sb("sel", [P, RING, P])
        own = ph.sb("own", [P, 2, C + AW])
        z = ph.sb("z", [P, 2, C + AW])
        ps_g = ph.psum("g", [P, 2 * BANK])
        ps_a = ph.psum("a", [P, 2 * BANK])
        STEPS = ITEMS // RING
        with nc.Block() as block:
            @block.gpsimd
            def _(pool):
                pool.sem_inc(begun, 1)

                def body(k, first):
                    for u in range(RING):
                        i = k * RING + u
                        if u % BATCH == 0:
                            if not first:
                                pool.wait_ge(sel_ready, i + BATCH - RING)
                            pool.tensor_copy(stage[:, u:u + BATCH], g.src_item[:, bass.ds(i, BATCH)]).then_inc(staged, 1)
                            pool.wait_ge(staged, k * (RING // BATCH) + u // BATCH + 1)
                        if not first:
                            pool.wait_ge(item_used, i + 1 - RING)
                        pool.sem_inc(issued, 1)
                        pool.wait_ge(begun, 1)
                        pool.indirect_dma_start(rows[:, u, :], None, g.node_rows,
                                                bass.IndirectOffsetOnAxis(stage[:, u:u + 1], 0)).then_inc(landed[u], 16)
                peeled(pool, STEPS, body)

            @block.sync
            def _(sp):
                def load(b, u):
                    sp.dma_start(own[:, u, 0:C], g.node_rows[bass.ds(b * P, P), 0:C]).then_inc(own_loaded[u], 16)
                    sp.dma_start(own[:, u, C:C + AW], g.own[bass.ds(b * P, P), :]).then_inc(own_loaded[u], 16)

                def body(k, first):
                    for u in range(2):
                        if not first:
                            sp.wait_ge(opened, 2 * k + u - 1)
                        load(2 * k + u, u)
                        sp.wait_ge(own_loaded[u], 32 * k + 32)
                        sp.sem_inc(own_relay, 1)
                peeled(sp, NODE_BLOCKS // 2, body)

            @block.vector
            def _(dve):
                def body(k, first):
                    for u in range(RING):
                        i = k * RING + u
                        if not first:
                            dve.wait_ge(item_used, i + 1 - RING)
                        dve.tensor_scalar(sel_w[:, u, :], g.iota[:, :], col(g.dst_item, i), col(g.w_item, i), ALU.is_equal, ALU.mult)
                        dve.tensor_scalar(sel[:, u, :], g.iota[:, :], col(g.dst_item, i), None, ALU.is_equal)
                        ee = g.ee_item[:, bass.ds(i, 1), :].rearrange("p o h -> p (o h)")
                        dve.tensor_copy(att[:, u, C:AW], ee)
                        dve.wait_ge(landed[u], 16 * k + 16)
                        dve.tensor_tensor(att[:, u, 0:C].rearrange("p (h d) -> p h d", h=H), rows[:, u, C:2 * C].rearrange("p (h d) -> p h d", h=H),
                                          ee.unsqueeze(2).to_broadcast([P, H, GAT_D]), ALU.mult).then_inc(sel_ready, 1)
                peeled(dve, STEPS, body)

            @block.tensor
            def _(pe):
                def open_block(b, bank, slot):
                    pe.wait_ge(own_relay, b + 1)
                    pe.matmul(ps_g[:, bass.ds(bank, C)], g.ident[:, :], own[:, slot, 0:C].rearrange("p o c -> p (o c)"), start=True, stop=False)
                    pe.matmul(ps_a[:, bass.ds(bank, AW)], g.ident[:, :], own[:, slot, C:C + AW].rearrange("p o c -> p (o c)"), start=True, stop=False).then_inc(opened, 1)

                def end_block(bank):
                    pe.matmul(ps_g[:, bass.ds(bank, C)], g.zrow_bf[0:1, 0:P], g.zrow_bf[0:1, 0:C], start=False, stop=True)
                    pe.matmul(ps_a[:, bass.ds(bank, AW)], g.zrow_bf[0:1, 0:P], g.zrow_bf[0:1, 0:AW], start=False, stop=True).then_inc(sum_ready, 1)

                open_block(0, 0, slice(0, 1))

                def add(u, to, att_to):
                    pe.matmul(ps_g[:, to], sel_w[:, u, :], rows[:, u, 0:C], start=False, stop=False, skip_group_check=True)
                    pe.matmul(ps_a[:, att_to], sel[:, u, :], att[:, u, :], start=False, stop=False,
                              skip_group_check=True).then_inc(item_used, 1)

                def one(k, u, first):
                    i = k * RING + u
                    code = pe.value_load(g.item_code[0:1, bass.ds(i, 1)], min_val=0, max_val=2 * NODE_BLOCKS - 1)
                    if not (first and u == 0):
                        with pe.If(code % 2):
                            now = pe.value_load(g.item_code[0:1, bass.ds(i, 1)], min_val=3, max_val=2 * NODE_BLOCKS - 1)
                            b = pe.snap(now // 2)
                            end_block(((b + 1) % 2) * BANK)
                            pe.wait_ge(sum_kept, b)
                            open_block(b, (b % 2) * BANK, bass.ds(b % 2, 1))
                    bank = ((code // 2) % 2) * BANK
                    pe.wait_ge(sel_ready, i + 1)
                    add(u, bass.ds(bank, C), bass.ds(bank, AW))

                def body(k, first):
                    for at in range(0, RING, BATCH):
                        i = k * RING + at
                        a = pe.value_load(g.item_code[0:1, bass.ds(i, 1)], min_val=0, max_val=2 * NODE_BLOCKS - 1)
                        z = pe.value_load(g.item_code[0:1, bass.ds(i + BATCH - 1, 1)], min_val=0, max_val=2 * NODE_BLOCKS - 1)
                        with pe.If(z - a):
                            for u in range(at, at + BATCH):
                                one(k, u, first)
                        with pe.Else():
                            with pe.If((a // 2) % 2):
                                for u in range(at, at + BATCH):
                                    pe.wait_ge(sel_ready, k * RING + u + 1)
                                    add(u, slice(BANK, BANK + C), slice(BANK, BANK + AW))
                            with pe.Else():
                                for u in range(at, at + BATCH):
                                    pe.wait_ge(sel_ready, k * RING + u + 1)
                                    add(u, slice(0, C), slice(0, AW))
                peeled(pe, STEPS, body)
                end_block(((NODE_BLOCKS - 1) % 2) * BANK)

            @block.scalar
            def _(act):
                act.sem_inc(sum_kept, 1)

                def body(k, first):
                    for u in range(2):
                        b = 2 * k + u
                        act.wait_ge(sum_ready, b + 1)
                        if not first:
                            act.wait_ge(sum_stored[u], 16 * k)
                        act.activation(z[:, u, 0:C], ps_g[:, u * BANK:u * BANK + C], ACT.Copy)
                        act.activation(z[:, u, C:C + AW], ps_a[:, u * BANK:u * BANK + AW], ACT.Copy).then_inc(sum_kept, 1)
                        act.wait_ge(sum_kept, b + 2)
                        act.dma_start(g.sums[bass.ds(b * P, P), :], z[:, u, :]).then_inc(sum_stored[u], 16)
                peeled(act, NODE_BLOCKS // 2, body)
                for u in range(2):
                    act.wait_ge(sum_stored[u], 16 * (NODE_BLOCKS // 2))


def finish_gnn(nc, g):
    H = GAT_HEADS
    AW = C + H
    with phase(nc, "fin") as ph:
        w_loaded, root_in, root_out, step, bias_in, bias_done, w_ready, ones_set = (
            ph.sem(s) for s in ("w_loaded", "root_in", "root_out", "step", "bias_in", "bias_done", "w_ready", "ones_set"))
        loaded = [ph.sem("loaded0"), ph.sem("loaded1")]
        divided, turned, kept, out_done, added, chain = (ph.sem(s) for s in ("divided", "turned", "kept", "out_done", "added", "chain"))
        wp = ph.sb("wp", [P, KC, C])
        ws = ph.sb("ws", [P, KC, C])
        scale = ph.sb("scale", [P, C])
        var = ph.sb("var", [P, C])
        bgat = ph.sb("bgat", [P, KC])
        vecs = ph.sb("vecs", [1, 5, C])
        z = ph.sb("z", [P, 2, C + AW])
        xn = ph.sb("xn", [P, 2, C])
        rden = ph.sb("rden", [P, 2, H])
        at = ph.sb("at", [P, 2, C])
        cv = ph.sb("cv", [P, 2, C])
        tt = ph.sb("tt", [P, 2, C])
        y = ph.sb("y", [P, 2, C])
        ps_v = ph.psum("v", [P, C])
        ps_t = [ph.psum(f"t{u}", [P, C]) for u in range(2)]
        ps_o = [ph.psum(f"o{u}", [P, C]) for u in range(2)]
        STEPS = NODE_BLOCKS // 2
        with nc.Block() as block:
            @block.sync
            def _(sp):
                load_all(sp, w_loaded, [
                    (wp[:, :, :], by_rows(g.given["L1_gnn_W_proj"])), (bgat[:, :], columns(g.given["L1_gnn_b_gat"])),
                    (scale[:, :], every(g.given["L1_gnn_bn_gamma"])), (var[:, :], every(g.given["L1_gnn_bn_var"])),
                    (vecs[:, 0, :], row(g.given["L1_gnn_b_gcn"])), (vecs[:, 1, :], row(g.given["L1_gnn_b_proj"])),
                    (vecs[:, 2, :], row(g.given["L1_gnn_bn_mean"])), (vecs[:, 3, :], row(g.given["L1_gnn_bn_beta"]))])

                def body(k, first):
                    for u in range(2):
                        b = 2 * k + u
                        if not first:
                            sp.wait_ge(added, b - 1)
                        sp.dma_start(z[:, u, :], g.sums[bass.ds(b * P, P), :]).then_inc(loaded[u], 16)
                        sp.dma_start(xn[:, u, :], g.xn_rows[bass.ds(b * P, P), :]).then_inc(loaded[u], 16)
                peeled(sp, STEPS, body)

            @block.scalar
            def _(act):
                act.wait_ge(root_in, 1)
                act.activation(var[:, :], var[:, :], ACT.Sqrt).then_inc(root_out, 1)

                def body(k, first):
                    for u in range(2):
                        b = 2 * k + u
                        act.wait_ge(turned, b + 1)
                        if not first:
                            act.wait_ge(out_done, b - 1)
                        act.activation(tt[:, u, :], ps_t[u][:, :], ACT.Copy).then_inc(kept, 1)
                peeled(act, STEPS, body)

            @block.tensor
            def _(pe):
                pe.wait_ge(w_loaded, 16 * 8)
                for c in range(KC):
                    mm = pe.matmul(ps_v[0:1, :], bgat[:, c:c + 1], wp[:, c, :], start=(c == 0), stop=(c == KC - 1))
                mm.then_inc(bias_done, 1)
                pe.wait_ge(w_ready, 1)

                def project(b, u, first):
                    pe.wait_ge(kept, b + 1)
                    if not first:
                        pe.wait_ge(added, b - 1)
                    for c in range(KC):
                        pe.matmul(ps_o[u][:, :], tt[:, u, c * P:(c + 1) * P], ws[:, c, :], start=(c == 0), stop=False)
                    pe.matmul(ps_o[u][:, :], g.ones[0:1, :], vecs[:, 4, :], start=False, stop=True).then_inc(out_done, 1)

                def body(k, first):
                    for u in range(2):
                        b = 2 * k + u
                        pe.wait_ge(divided, b + 1)
                        if not first:
                            pe.wait_ge(kept, b - 1)
                        for c in range(KC):
                            mm = pe.transpose(ps_t[u][:, c * P:(c + 1) * P], at[:, u, c * P:(c + 1) * P], g.ident[:, :])
                        mm.then_inc(turned, 1)
                        if u == 1:
                            project(b - 1, 0, first)
                    project(2 * k + 1, 1, first)
                peeled(pe, STEPS, body)

            @block.vector
            def _(dve):
                n = Count()

                def done(op):
                    op.then_inc(step, 1)
                    dve.wait_ge(step, n.up())

                dve.wait_ge(w_loaded, 16 * 8)
                dve.tensor_scalar(var[:, :], var[:, :], EPS, None, ALU.add).then_inc(root_in, 1)
                dve.wait_ge(root_out, 1)
                done(dve.reciprocal(var[:, :], var[:, :]))
                done(dve.tensor_tensor(scale[:, :], scale[:, :], var[:, :], ALU.mult))
                for c in range(KC):
                    dve.tensor_tensor(ws[:, c, :], wp[:, c, :], scale[:, :], ALU.mult)
                done(dve.tensor_tensor(vecs[:, 4, :], vecs[:, 0, :], vecs[:, 1, :], ALU.add))
                done(dve.tensor_tensor(vecs[:, 4, :], vecs[:, 4, :], vecs[:, 2, :], ALU.subtract))
                dve.wait_ge(bias_done, 1)
                done(dve.tensor_tensor(vecs[:, 4, :], vecs[:, 4, :], ps_v[0:1, :], ALU.add))
                done(dve.tensor_tensor(vecs[:, 4, :], vecs[:, 4, :], scale[0:1, :], ALU.mult))
                dve.tensor_tensor(vecs[:, 4, :], vecs[:, 4, :], vecs[:, 3, :], ALU.add).then_inc(w_ready, 1)

                def body(k, first):
                    base = 6 * k
                    for u in range(2):
                        b = 2 * k + u
                        dve.wait_ge(loaded[u], 32 * k + 32)
                        if not first:
                            dve.wait_ge(turned, b - 1)
                        dve.reciprocal(rden[:, u, :], z[:, u, 2 * C:2 * C + H]).then_inc(chain, 1)
                        dve.scalar_tensor_tensor(cv[:, u, :], z[:, u, 0:C], col(g.dinv, b), scale[:, :], ALU.mult, ALU.mult)
                        dve.wait_ge(chain, base + u + 1)
                        dve.tensor_tensor(at[:, u, :].rearrange("p (h d) -> p h d", h=H), z[:, u, C:2 * C].rearrange("p (h d) -> p h d", h=H),
                                          rden[:, u, :].unsqueeze(2).to_broadcast([P, H, GAT_D]), ALU.mult).then_inc(divided, 1)
                    for u in range(2):
                        b = 2 * k + u
                        dve.wait_ge(out_done, b + 1)
                        dve.tensor_tensor(y[:, u, :], cv[:, u, :], ps_o[u][:, :], ALU.add).then_inc(chain, 1)
                        dve.wait_ge(chain, base + 2 + 2 * u + 1)
                        dve.scalar_tensor_tensor(y[:, u, :], y[:, u, :], 0.0, xn[:, u, :], ALU.max, ALU.add).then_inc(chain, 1)
                        dve.wait_ge(chain, base + 2 + 2 * u + 2)
                        dve.tensor_tensor(x_block(g, b), x_block(g, b), y[:, u, :], ALU.add).then_inc(added, 1)
                peeled(dve, STEPS, body)


LOT = 23
FETCH_LOTS = -(-PER // LOT)
CTX_LOTS = 16
assert CTX_LOTS % 2 == 0 and FETCH_LOTS % 2 == 0


class SourceTerms:

    def __init__(self, ph, first, count):
        self.first, self.count = first, count
        self.begin = first * LOT
        self.end = min((first + count) * LOT, PER)
        self.loaded, self.staged, self.issued = ph.sem("idx_loaded"), ph.sem("idx_staged"), ph.sem("idx_issued")
        self.landed = [ph.sem(f"terms_landed{u}") for u in range(2)]
        self.stored = [ph.sem(f"terms_stored{u}") for u in range(2)]
        self.src = ph.sb("src_part", [P, self.end - self.begin], I32)
        self.stage = ph.sb("idx_stage", [P, 2, LOT], U32)
        self.lots = ph.sb("lots", [P, 2, LOT, GAT_HEADS])

    def load(self, sp, g):
        flat = g.srcP.rearrange("t p -> (t p)").rearrange("(q j) -> q j", q=P)
        sp.dma_start(self.src[:, :], flat[:, self.begin:self.end]).then_inc(self.loaded, 16)

    def run(self, pool, g):
        steps = self.count // 2

        def store(u, at):
            pool.dma_start(g.edge_terms[:, bass.ds(at * GAT_HEADS, LOT * GAT_HEADS)],
                           self.lots[:, u, :, :].rearrange("p i h -> p (i h)")).then_inc(self.stored[u], 16)

        def body(k, first, last):
            for u in range(2):
                lot = 2 * k + u
                at = lot * LOT
                if last and u == 1:
                    at = self.end - self.begin - LOT
                if not first:
                    pool.wait_ge(self.stored[u], 16 * k)
                pool.tensor_copy(self.stage[:, u, :], self.src[:, bass.ds(at, LOT)]).then_inc(self.staged, 1)
                pool.wait_ge(self.staged, lot + 1)
                pool.sem_inc(self.issued, 1)
                pool.wait_ge(self.loaded, 16)
                for i in range(LOT):
                    pool.indirect_dma_start(self.lots[:, u, i, :], None, g.src_terms,
                                            bass.IndirectOffsetOnAxis(self.stage[:, u, i:i + 1], 0)).then_inc(self.landed[u], 16)
                if not (first and u == 0):
                    v = 1 - u
                    pool.wait_ge(self.landed[v], 16 * LOT * (k if u == 0 else k + 1))
                    store(v, self.begin + (lot - 1) * LOT)

        pool.wait_ge(self.loaded, 16)
        peeled_both(pool, steps, body)
        pool.wait_ge(self.landed[1], 16 * LOT * steps)
        pool.wait_ge(self.stored[0], 16 * steps)
        store(1, self.end - LOT)
        pool.wait_ge(self.stored[1], 16 * steps)


def context1(nc, g):
    with phase(nc, "ctx1") as ph:
        loaded, used = [ph.sem("loaded0"), ph.sem("loaded1")], ph.sem("used")
        w_loaded, low_ready, high_ready, exp_ready, keys_ready, sums_used, sums_ready, ones_set, step = (
            ph.sem(s) for s in ("w_loaded", "low_ready", "high_ready", "exp_ready", "keys_ready", "sums_used", "sums_ready", "ones_set", "step"))
        xt = ph.sb("xt", [P, 2, KC * ROWS])
        wkv = ph.sb("wkv", [P, KC, 2 * C])
        bk = ph.sb("bk", [P, C])
        bv = ph.sb("bv", [P, C])
        kb = ph.sb("kb", [P, 2, GROUP, C])
        low = ph.sb("low", [P, 2, GROUP, C])
        ex = ph.sb("ex", [P, 2, GROUP, C])
        fk = ph.sb("fk", [P, 2, GROUP, C])
        v1 = ph.sb("v1", [P, 2, GROUP, KC, P + 1])
        ksum = ph.sb("ksum", [P, KC])
        ps = [[ph.psum(f"kv{u}{j}", [P, 2 * C]) for j in range(GROUP)] for u in range(2)]
        ps_ctx = [ph.psum(f"ctx{c}", [P, P + 1]) for c in range(KC)]
        fetch = SourceTerms(ph, 0, CTX_LOTS)
        with nc.Block() as block:
            @block.sync
            def _(sp):
                fetch.load(sp, g)
                load_all(sp, w_loaded, [(wkv[:, :, 0:C], by_rows(g.given["L1_mix_Wk"])), (wkv[:, :, C:2 * C], by_rows(g.given["L1_mix_Wv"])),
                                        (bk[:, :], every(g.given["L1_mix_bk"])), (bv[:, :], every(g.given["L1_mix_bv"]))])
                load_groups(sp, g, xt, loaded, used)

            @block.gpsimd
            def _(pool):
                pool.memset(v1[:, :, :, :, P:P + 1].rearrange("p u j c o -> p (u j c) o"), 1.0).then_inc(ones_set, 1)
                fetch.run(pool, g)

            @block.tensor
            def _(pe):
                pe.wait_ge(w_loaded, 64)
                pe.wait_ge(ones_set, 1)
                for c in range(KC):
                    pe.matmul(ps_ctx[c][:, :], g.zrow[0:1, 0:P], g.zrow[0:1, 0:P + 1], start=True, stop=False)

                def add(gi, u):
                    pe.wait_ge(keys_ready, gi + 1)
                    for j in range(GROUP):
                        for c in range(KC):
                            mm = pe.matmul(ps_ctx[c][:, :], fk[:, u, j, c * P:(c + 1) * P], v1[:, u, j, c, :],
                                           start=False, stop=False, skip_group_check=True)
                    mm.then_inc(sums_used, 1)

                def body(k, first):
                    for u in range(2):
                        gi = 2 * k + u
                        pe.wait_ge(loaded[u], 16 * k + 16)
                        if not first:
                            pe.wait_ge(low_ready, gi - 1)
                        for j in range(GROUP):
                            for c in range(KC):
                                mm = pe.matmul(ps[u][j][:, :], chunk(xt, u, c, j), wkv[:, c, :], start=(c == 0), stop=(c == KC - 1))
                        mm.then_inc(used, 1)
                        if not (first and u == 0):
                            add(gi - 1, 1 - u)
                peeled(pe, PAIRS, body)
                add(GROUPS - 1, 1)
                for c in range(KC):
                    mm = pe.matmul(ps_ctx[c][:, :], g.zrow[0:1, 0:P], g.zrow[0:1, 0:P + 1], start=False, stop=True)
                mm.then_inc(sums_ready, 1)

            @block.scalar
            def _(act):
                def body(k, first):
                    for u in range(2):
                        gi = 2 * k + u
                        act.wait_ge(low_ready, gi + 1)
                        if not first:
                            act.wait_ge(keys_ready, gi - 1)
                        for j in range(GROUP):
                            op = act.activation(ex[:, u, j, :], low[:, u, j, :], ACT.Exp, bias=col(g.maskbias, gi * GROUP + j))
                        op.then_inc(exp_ready, 1)
                peeled(act, PAIRS, body)

            @block.vector
            def _(dve):
                dve.wait_ge(w_loaded, 64)

                def finish(gi, u):
                    dve.wait_ge(exp_ready, gi + 1)
                    dve.wait_ge(high_ready, gi + 1)
                    dve.tensor_tensor(fk[:, u, :, :], fk[:, u, :, :], ex[:, u, :, :], ALU.add).then_inc(keys_ready, 1)

                def body(k, first):
                    for u in range(2):
                        gi = 2 * k + u
                        dve.wait_ge(used, gi + 1)
                        if not first:
                            dve.wait_ge(sums_used, gi - 1)
                            dve.wait_ge(exp_ready, gi - 1)
                        for j in range(GROUP):
                            dve.tensor_tensor(v1[:, u, j, :, 0:P], ps[u][j][:, C:2 * C].rearrange("p (c d) -> p c d", c=KC),
                                              bv[:, :].rearrange("p (c d) -> p c d", c=KC), ALU.add).then_inc(step, 1)
                            dve.tensor_tensor(kb[:, u, j, :], ps[u][j][:, 0:C], bk[:, :], ALU.add).then_inc(step, 1)
                        dve.wait_ge(step, 2 * GROUP * (gi + 1))
                        dve.tensor_scalar(low[:, u, :, :], kb[:, u, :, :], 0.0, None, ALU.min).then_inc(low_ready, 1)
                        for j in range(GROUP):
                            op = dve.tensor_scalar(fk[:, u, j, :], kb[:, u, j, :], 0.0, col(g.maskcol, gi * GROUP + j), ALU.max, ALU.mult)
                        op.then_inc(high_ready, 1)
                        if not (first and u == 0):
                            finish(gi - 1, 1 - u)
                peeled(dve, PAIRS, body)
                finish(GROUPS - 1, 1)
                dve.wait_ge(sums_ready, 1)
                for c in range(KC):
                    dve.tensor_tensor(g.kv[:, c, :], ps_ctx[c][:, 0:P], g.same_head[:, :], ALU.mult)
                    dve.tensor_copy(ksum[:, c:c + 1], ps_ctx[c][:, P:P + 1]).then_inc(step, 1)
                dve.wait_ge(step, 2 * GROUP * GROUPS + KC)
                for c in range(KC):
                    dve.tensor_scalar(g.ks[:, c, :], g.same_head[:, :], ksum[:, c:c + 1], None, ALU.mult)


def mix1(nc, g):
    M = FF // P
    with phase(nc, "mix1") as ph:
        S = ph.sem
        loaded, rows_loaded = [S("loaded0"), S("loaded1")], [S("rows_loaded0"), S("rows_loaded1")]
        w_loaded, w_ready, bias_done, bias_ready, var_ready, root_ready = (
            S(s) for s in ("w_loaded", "w_ready", "bias_done", "bias_ready", "var_ready", "root_ready"))
        q_done, low_ready, exp_ready, phi_ready, nd_done, att_ready, o_done = (
            S(s) for s in ("q_done", "low_ready", "exp_ready", "phi_ready", "nd_done", "att_ready", "o_done"))
        x1_ready, turned, kept, h_done, h_kept, f_done, added, step, stats_seen = (
            S(s) for s in ("x1_ready", "turned", "kept", "h_done", "h_kept", "f_done", "added", "step", "stats_seen"))
        xt = ph.sb("xt", [P, 2, KC * ROWS])
        xr = ph.sb("xr", [P, 2, GROUP, C])
        wq = ph.sb("wq", [P, KC, C])
        bq = ph.sb("bq", [P, KC])
        wo = ph.sb("wo", [P, KC, C])
        w1 = ph.sb("w1", [P, KC, FF])
        w2 = ph.sb("w2", [P, M, C])
        b1 = ph.sb("b1", [P, M])
        g1 = ph.sb("g1", [P, KC])
        be1 = ph.sb("be1", [P, KC])
        vec = ph.sb("vec", [1, 2, C])
        ln = ph.sb("ln", [P, 4, C])
        qb = ph.sb("qb", [P, KC, ROWS])
        low = ph.sb("low", [P, KC, ROWS])
        fq = ph.sb("fq", [P, KC, ROWS])
        rec = ph.sb("rec", [P, KC, ROWS])
        at = ph.sb("at", [P, KC, ROWS])
        r = ph.sb("r", [P, GROUP, C])
        x1n = ph.sb("x1n", [P, GROUP, C])
        x1 = ph.sb("x1", [P, GROUP, C])
        x1t = ph.sb("x1t", [P, KC, ROWS])
        ht = ph.sb("ht", [P, M, ROWS])
        st = ph.sb("st", [P, GROUP, 6])
        mv = ph.sb("mv", [P, GROUP, 2])
        ve = ph.sb("ve", [P, GROUP])
        rs = ph.sb("rs", [P, GROUP])
        ps_q = ph.psum("q", [P, KC, ROWS])
        ps_n = ph.psum("n", [P, KC, ROWS])
        ps_d = ph.psum("d", [P, KC, ROWS])
        ps_o = ph.psum("o", [P, GROUP, C])
        ps_t = ph.psum("t", [P, KC, ROWS])
        ps_h = [ph.psum(f"h{i}", [P, 2, ROWS]) for i in range(2)]
        ps_f = ph.psum("f", [P, GROUP, C])
        fetch = SourceTerms(ph, CTX_LOTS, FETCH_LOTS - CTX_LOTS)
        with nc.Block() as block:
            @block.sync
            def _(sp):
                fetch.load(sp, g)
                load_all(sp, w_loaded, [
                    (wq[:, :, :], by_rows(g.given["L1_mix_Wq"])), (wo[:, :, :], by_rows(g.given["L1_mix_Wo"])),
                    (w1[:, :, :], by_rows(g.given["L1_mix_W1"])), (w2[:, :, :], by_rows(g.given["L1_mix_W2"])),
                    (bq[:, :], columns(g.given["L1_mix_bq"])), (b1[:, :], columns(g.given["L1_mix_b1"])),
                    (g1[:, :], columns(g.given["L1_mix_ln1_g"])), (be1[:, :], columns(g.given["L1_mix_ln1_b"])),
                    (vec[:, 0, :], row(g.given["L1_mix_bo"])), (vec[:, 1, :], row(g.given["L1_mix_b2"])),
                    (ln[:, 0, :], every(g.given["L1_mix_ln1_g"])), (ln[:, 1, :], every(g.given["L1_mix_ln1_b"])),
                    (ln[:, 2, :], every(g.given["L1_mix_ln2_g"])), (ln[:, 3, :], every(g.given["L1_mix_ln2_b"]))])

                def body(k, first):
                    for u in range(2):
                        gi = 2 * k + u
                        if not first:
                            sp.wait_ge(q_done, gi - 1)
                            sp.wait_ge(x1_ready, gi - 1)
                        sp.dma_start(xt[:, u, :], g.xn_turned[bass.ds(gi, 1), :, :].rearrange("o p c -> (o p) c")).then_inc(loaded[u], 16)
                        sp.dma_start(xr[:, u, :, :], g.xn_rows[bass.ds(gi * ROWS, ROWS), :].rearrange("(j p) c -> p j c", p=P)).then_inc(rows_loaded[u], 16)
                peeled(sp, PAIRS, body)

            @block.gpsimd
            def _(pool):
                fetch.run(pool, g)

            @block.tensor
            def _(pe):
                pe.wait_ge(w_loaded, 16 * 14)
                for m in range(M):
                    for c in range(KC):
                        mm = pe.matmul(ps_q[:, 0, m:m + 1], w1[:, c, m * P:(m + 1) * P], be1[:, c:c + 1], start=(c == 0), stop=(c == KC - 1))
                mm.then_inc(bias_done, 1)
                pe.wait_ge(w_ready, 1)

                def queries(gi, u, k16, start):
                    pe.wait_ge(loaded[u], k16)
                    if not start:
                        pe.wait_ge(low_ready, gi)
                    for m in range(KC):
                        for c in range(KC):
                            mm = pe.matmul(ps_q[:, m, :], wq[:, c, m * P:(m + 1) * P], chunk(xt, u, c), start=(c == 0), stop=(c == KC - 1))
                    mm.then_inc(q_done, 1)

                def attend(gi, start):
                    pe.wait_ge(phi_ready, gi + 1)
                    if not start:
                        pe.wait_ge(att_ready, gi)
                    for m in range(KC):
                        pe.matmul(ps_n[:, m, :], g.kv[:, m, :], fq[:, m, :], start=True, stop=True)
                        mm = pe.matmul(ps_d[:, m, :], g.ks[:, m, :], fq[:, m, :], start=True, stop=True)
                    mm.then_inc(nd_done, 1)

                def out(gi, start):
                    pe.wait_ge(att_ready, gi + 1)
                    if not start:
                        pe.wait_ge(x1_ready, gi)
                    for j in range(GROUP):
                        for c in range(KC):
                            pe.matmul(ps_o[:, j, :], at[:, c, j * P:(j + 1) * P], wo[:, c, :], start=(c == 0), stop=False)
                        mm = pe.matmul(ps_o[:, j, :], g.ones[0:1, :], vec[:, 0, :], start=False, stop=True)
                    mm.then_inc(o_done, 1)

                def turn(gi, start):
                    pe.wait_ge(x1_ready, gi + 1)
                    if not start:
                        pe.wait_ge(kept, gi)
                    for j in range(GROUP):
                        for c in range(KC):
                            mm = pe.transpose(ps_t[:, c, j * P:(j + 1) * P], x1n[:, j, c * P:(c + 1) * P], g.ident[:, :])
                    mm.then_inc(turned, 1)

                def hidden(gi, half, start):
                    pe.wait_ge(kept, gi + 1)
                    for i in range(2):
                        if not (start and half == 0):
                            pe.wait_ge(h_kept, 4 * gi + 2 * half + i - 1)
                        for m in (4 * half + 2 * i, 4 * half + 2 * i + 1):
                            for c in range(KC):
                                mm = pe.matmul(ps_h[i][:, m % 2, :], w1[:, c, m * P:(m + 1) * P], x1t[:, c, :], start=(c == 0), stop=(c == KC - 1))
                        mm.then_inc(h_done, 1)

                def last(gi, start):
                    pe.wait_ge(h_kept, 4 * gi + 4)
                    if not start:
                        pe.wait_ge(added, gi)
                    for j in range(GROUP):
                        for m in range(M):
                            pe.matmul(ps_f[:, j, :], ht[:, m, j * P:(j + 1) * P], w2[:, m, :], start=(m == 0), stop=False)
                        mm = pe.matmul(ps_f[:, j, :], g.ones[0:1, :], vec[:, 1, :], start=False, stop=True)
                    mm.then_inc(f_done, 1)

                def body(k, first):
                    for u in range(2):
                        gi = 2 * k + u
                        start, second = first and u == 0, first and u == 1
                        queries(gi, u, 16 * k + 16, start)
                        if not start:
                            hidden(gi - 1, 0, second)
                        attend(gi, start)
                        if not start:
                            hidden(gi - 1, 1, second)
                        out(gi, start)
                        if not start:
                            last(gi - 1, second)
                        turn(gi, start)
                peeled(pe, PAIRS, body)
                hidden(GROUPS - 1, 0, False)
                hidden(GROUPS - 1, 1, False)
                last(GROUPS - 1, False)

            @block.scalar
            def _(act):
                act.wait_ge(bias_ready, 1)

                def square_root(norms):
                    act.wait_ge(var_ready, norms)
                    act.activation(rs[:, :], ve[:, :], ACT.Sqrt).then_inc(root_ready, 1)

                def bend(gi, half, start):
                    for i in range(2):
                        act.wait_ge(h_done, 4 * gi + 2 * half + i + 1)
                        if half == 0 and i == 0 and not start:
                            act.wait_ge(f_done, gi)
                        for m in (4 * half + 2 * i, 4 * half + 2 * i + 1):
                            op = act.activation(ht[:, m, :], ps_h[i][:, m % 2, :], ACT.Relu, bias=b1[:, m:m + 1])
                        op.then_inc(h_kept, 1)

                def body(k, first):
                    for u in range(2):
                        gi = 2 * k + u
                        start, second = first and u == 0, first and u == 1
                        act.wait_ge(low_ready, gi + 1)
                        act.activation(low[:, :, :], low[:, :, :], ACT.Exp).then_inc(exp_ready, 1)
                        if not start:
                            bend(gi - 1, 0, second)
                            bend(gi - 1, 1, second)
                        square_root(1 if start else 2 * gi)
                        act.wait_ge(turned, gi + 1)
                        act.activation(x1t[:, :, :], ps_t[:, :, :], ACT.Copy).then_inc(kept, 1)
                        if not start:
                            square_root(2 * gi + 1)
                peeled(act, PAIRS, body)
                bend(GROUPS - 1, 0, False)
                bend(GROUPS - 1, 1, False)
                square_root(2 * GROUPS)

            @block.vector
            def _(dve):
                dve.wait_ge(bias_done, 1)
                dve.tensor_tensor(b1[:, :], b1[:, :], ps_q[:, 0, 0:M], ALU.add).then_inc(bias_ready, 1)
                for c in range(KC):
                    op = dve.tensor_scalar(w1[:, c, :], w1[:, c, :], g1[:, c:c + 1], None, ALU.mult)
                op.then_inc(w_ready, 1)

                def rows_norm(n, src, dst, norms):
                    for j in range(GROUP):
                        dve.bn_stats(st[:, j, :], src[:, j, :]).then_inc(step, 1)
                    dve.wait_ge(step, n.up(GROUP))
                    dve.sem_inc(stats_seen, 1)
                    for j in range(GROUP):
                        dve.bn_aggr(mv[:, j, :], st[:, j, :]).then_inc(step, 1)
                    dve.wait_ge(step, n.up(GROUP))
                    dve.tensor_scalar(ve[:, :], mv[:, :, 1], EPS, None, ALU.add).then_inc(var_ready, 1)
                    dve.wait_ge(root_ready, norms)
                    dve.reciprocal(rs[:, :], rs[:, :]).then_inc(step, 1)
                    dve.wait_ge(step, n.up())
                    for j in range(GROUP):
                        op = dve.tensor_scalar(dst[:, j, :], src[:, j, :], mv[:, j, 0:1], rs[:, j:j + 1], ALU.subtract, ALU.mult)
                    return op

                def gain(t, i):
                    return ln[:, i, :].unsqueeze(1).to_broadcast([P, GROUP, C])

                def attention_part(gi, u, k16, n, start):
                    dve.wait_ge(q_done, gi + 1)
                    for m in range(KC):
                        op = dve.tensor_scalar(qb[:, m, :], ps_q[:, m, :], bq[:, m:m + 1], None, ALU.add)
                    op.then_inc(step, 1)
                    dve.wait_ge(step, n.up())
                    dve.tensor_scalar(low[:, :, :], qb[:, :, :], 0.0, None, ALU.min).then_inc(low_ready, 1)
                    dve.wait_ge(exp_ready, gi + 1)
                    if not start:
                        dve.wait_ge(nd_done, gi)
                    dve.scalar_tensor_tensor(fq[:, :, :], qb[:, :, :], 0.0, low[:, :, :], ALU.max, ALU.add).then_inc(phi_ready, 1)
                    dve.wait_ge(nd_done, gi + 1)
                    dve.tensor_scalar(rec[:, :, :], ps_d[:, :, :], 1e-6, None, ALU.add).then_inc(step, 1)
                    dve.wait_ge(step, n.up())
                    dve.reciprocal(rec[:, :, :], rec[:, :, :]).then_inc(step, 1)
                    dve.wait_ge(step, n.up())
                    if not start:
                        dve.wait_ge(o_done, gi)
                    dve.tensor_tensor(at[:, :, :], rec[:, :, :], ps_n[:, :, :], ALU.mult).then_inc(att_ready, 1)

                def norm_part(gi, u, k16, n, norms, start, early):
                    dve.wait_ge(o_done, gi + 1)
                    dve.wait_ge(rows_loaded[u], k16)
                    if not early:
                        dve.wait_ge(added, gi - 1)
                    dve.tensor_tensor(r[:, :, :], xr[:, u, :, :], ps_o[:, :, :], ALU.add).then_inc(step, 1)
                    dve.wait_ge(step, n.up())
                    if not start:
                        dve.wait_ge(turned, gi)
                    rows_norm(n, r, x1n, norms).then_inc(x1_ready, 1)

                def mlp_part(gi, n, norms, x1_parts):
                    dve.wait_ge(f_done, gi + 1)
                    dve.wait_ge(x1_ready, x1_parts)
                    dve.tensor_tensor(r[:, :, :], x1[:, :, :], ps_f[:, :, :], ALU.add).then_inc(step, 1)
                    dve.wait_ge(step, n.up())
                    rows_norm(n, r, r, norms).then_inc(step, 1)
                    dve.wait_ge(step, n.up())
                    dve.tensor_tensor(r[:, :, :], r[:, :, :], gain(r, 2), ALU.mult).then_inc(step, 1)
                    dve.wait_ge(step, n.up())
                    dve.tensor_tensor(r[:, :, :], r[:, :, :], gain(r, 3), ALU.add).then_inc(step, 1)
                    dve.wait_ge(step, n.up())
                    at_x = g.x_sb[:, bass.ds(gi * GROUP, GROUP), :]
                    dve.tensor_tensor(at_x, at_x, r[:, :, :], ALU.add).then_inc(added, 1)

                def x1_part(gi, n):
                    dve.wait_ge(x1_ready, gi + 1)
                    dve.tensor_tensor(x1[:, :, :], x1n[:, :, :], gain(x1, 0), ALU.mult).then_inc(step, 1)
                    dve.wait_ge(step, n.up())
                    dve.tensor_tensor(x1[:, :, :], x1[:, :, :], gain(x1, 1), ALU.add).then_inc(step, 1)
                    dve.wait_ge(step, n.up())

                OWN = 1 + 2 + 1 + 5 + 2
                MLP = 1 + 5 + 3
                dve.wait_ge(w_loaded, 16 * 14)

                def body(k, first):
                    for u in range(2):
                        gi = 2 * k + u
                        start = first and u == 0
                        n = Count(0 if start else gi * OWN + (gi - 1) * MLP)
                        attention_part(gi, u, 16 * k + 16, n, start)
                        norm_part(gi, u, 16 * k + 16, n, 1 if start else 2 * gi, start, first)
                        if not start:
                            mlp_part(gi - 1, n, 2 * gi + 1, gi + 1)
                        x1_part(gi, n)
                peeled(dve, PAIRS, body)
                n = Count(GROUPS * OWN + (GROUPS - 1) * MLP)
                mlp_part(GROUPS - 1, n, 2 * GROUPS, GROUPS)


def select(nc, g):
    with phase(nc, "sel") as ph:
        loaded, counted, summed, step, rank_done, ok_seen = (
            ph.sem(s) for s in ("loaded", "counted", "summed", "step", "rank_done", "ok_seen"))
        br = ph.sb("br", [P, 1])
        w = ph.sb("w", [P, TILES])
        um = ph.sb("um", [P, TILES])
        hit = ph.sb("hit", [P, TILES])
        cnt = ph.sb("cnt", [P, 1])
        sign = ph.sb("sign", [P, 1])
        need = ph.sb("need", [P, 1])
        ok = ph.sb("ok", [P, 1], I32)
        bit = ph.sb("bit", [P, 1], I32)
        cur = ph.sb("cur", [P, 1], I32)
        cand = ph.sb("cand", [P, 1], I32)
        thr = ph.sb("thr", [P, 1])
        gt = ph.sb("gt", [P, TILES])
        eq = ph.sb("eq", [P, TILES])
        tot = ph.sb("tot", [P, TILES])
        run = ph.sb("run", [P, TILES])
        ps_c = ph.psum("c", [P, 1])
        ps_in = ph.psum("in", [P, TILES])
        ps_tot = ph.psum("tot", [P, TILES])
        BITS = 31
        with nc.Block() as block:
            @block.sync
            def _(sp):
                load_all(sp, loaded, [(br[:, :], every(g.given["L1_ffn_br"]))])

            @block.tensor
            def _(pe):
                with pe.Fori(0, BITS + 2) as k:
                    pe.wait_ge(counted, k + 1)
                    pe.matmul(ps_c[:, :], g.ones[:, :], cnt[:, :], start=True, stop=True).then_inc(summed, 1)
                pe.wait_ge(counted, BITS + 3)
                pe.matmul(ps_in[:, :], g.upper[:, :], eq[:, :], start=True, stop=True)
                pe.matmul(ps_tot[:, :], g.ones[:, :], eq[:, :], start=True, stop=True).then_inc(rank_done, 1)

            @block.vector
            def _(dve):
                n = Count()

                def done(op):
                    op.then_inc(step, 1)
                    dve.wait_ge(step, n.up())

                dve.wait_ge(loaded, 16)
                done(dve.tensor_scalar(w[:, :], g.router[:, :, 0], br[:, 0:1], None, ALU.add))
                done(dve.tensor_tensor(w[:, :], w[:, :], g.maskcol[:, :], ALU.mult))
                done(dve.tensor_tensor(w[:, :], w[:, :], g.maskbias[:, :], ALU.add))
                dve.tensor_scalar(hit[:, :], w[:, :], 0.0, 0.0, ALU.is_ge, ALU.add, accum_out=cnt[:, :]).then_inc(counted, 1)
                dve.wait_ge(summed, 1)
                done(dve.tensor_scalar(sign[:, :], ps_c[:, :], float(KEEP), None, ALU.is_ge))
                done(dve.tensor_scalar(need[:, :], sign[:, :], float(2 * KEEP - NODES - 1), float(NODES - KEEP + 1), ALU.mult, ALU.add))
                done(dve.tensor_scalar(sign[:, :], sign[:, :], 2.0, -1.0, ALU.mult, ALU.add))
                done(dve.tensor_scalar(um[:, :], w[:, :], sign[:, 0:1], None, ALU.mult))
                done(dve.tensor_tensor(um[:, :], um[:, :], g.maskcol[:, :], ALU.mult))
                done(dve.tensor_tensor(um[:, :], um[:, :], g.maskbias[:, :], ALU.add))
                done(dve.memset(bit[:, :], 1 << (BITS - 1)))
                done(dve.memset(cur[:, :], 0))
                base = n.n

                with dve.Fori(0, BITS) as k:
                    m = Count(base + 3 * k)
                    dve.tensor_tensor(cand[:, :], cur[:, :], bit[:, :], ALU.bitwise_or).then_inc(step, 1)
                    dve.wait_ge(step, m.up())
                    dve.tensor_scalar(hit[:, :], um[:, :], cand[:, :].bitcast(F32), 0.0, ALU.is_ge, ALU.add, accum_out=cnt[:, :]).then_inc(counted, 1)
                    dve.wait_ge(summed, k + 2)
                    dve.tensor_scalar(ok[:, :], ps_c[:, :], need[:, 0:1], None, ALU.is_ge).then_inc(step, 1)
                    dve.wait_ge(step, m.up())
                    dve.sem_inc(ok_seen, 1)
                    dve.copy_predicated(cur[:, :], ok[:, :], cand[:, :])
                    dve.tensor_scalar(bit[:, :], bit[:, :], 1, None, ALU.logical_shift_right).then_inc(step, 1)
                    dve.wait_ge(step, m.up())
                n = Count(base + 3 * BITS)
                done(dve.tensor_scalar(thr[:, :], cur[:, :].bitcast(F32), sign[:, 0:1], None, ALU.mult))
                dve.tensor_scalar(eq[:, :], w[:, :], thr[:, 0:1], None, ALU.is_equal)
                dve.tensor_scalar(gt[:, :], w[:, :], thr[:, 0:1], 0.0, ALU.is_gt, ALU.add, accum_out=cnt[:, :]).then_inc(counted, 1)
                dve.wait_ge(summed, BITS + 2)
                done(dve.tensor_scalar(need[:, :], ps_c[:, :], -1.0, float(KEEP), ALU.mult, ALU.add))
                dve.sem_inc(counted, 1)
                dve.wait_ge(rank_done, 1)
                done(dve.tensor_copy(tot[:, :], ps_tot[:, :]))
                done(dve.tensor_tensor_scan(run[:, :], g.ones[:, 0:TILES], tot[:, :], 0.0, ALU.mult, ALU.add))
                done(dve.tensor_tensor(run[:, :], run[:, :], tot[:, :], ALU.subtract))
                done(dve.tensor_tensor(run[:, :], run[:, :], ps_in[:, :], ALU.add))
                done(dve.scalar_tensor_tensor(run[:, :], run[:, :], need[:, 0:1], eq[:, :], ALU.is_lt, ALU.mult))
                done(dve.tensor_tensor(gt[:, :], gt[:, :], run[:, :], ALU.add))
                done(dve.tensor_tensor(w[:, :], w[:, :], g.maskcol[:, :], ALU.mult))
                dve.tensor_tensor(g.gain[:, :], w[:, :], gt[:, :], ALU.mult)


def ffn1(nc, g):
    M = FF // P
    with phase(nc, "ffn1") as ph:
        loaded, used = [ph.sem("loaded0"), ph.sem("loaded1")], ph.sem("used")
        w_loaded, h_done, h_kept, f_done, added = (ph.sem(s) for s in ("w_loaded", "h_done", "h_kept", "f_done", "added"))
        xt = ph.sb("xt", [P, 2, KC * ROWS])
        w1 = ph.sb("w1", [P, KC, FF])
        w2 = ph.sb("w2", [P, M, C])
        b1 = ph.sb("b1", [P, M])
        b2 = ph.sb("b2", [1, C])
        ht = ph.sb("ht", [P, 2, M, ROWS])
        ps_h = [ph.psum(f"h{i}", [P, 2, ROWS]) for i in range(4)]
        ps_f = [ph.psum(f"f{i}", [P, GROUP, C]) for i in range(2)]
        with nc.Block() as block:
            @block.sync
            def _(sp):
                load_all(sp, w_loaded, [(w1[:, :, :], by_rows(g.given["L1_ffn_w1"])), (w2[:, :, :], by_rows(g.given["L1_ffn_w2"])),
                                        (b1[:, :], columns(g.given["L1_ffn_b1"])), (b2[:, :], row(g.given["L1_ffn_b2"]))])
                load_groups(sp, g, xt, loaded, used)

            @block.tensor
            def _(pe):
                pe.wait_ge(w_loaded, 64)

                def last(gi, u, first):
                    pe.wait_ge(h_kept, 4 * gi + 4)
                    if not first:
                        pe.wait_ge(added, gi - 1)
                    for j in range(GROUP):
                        for m in range(M):
                            pe.matmul(ps_f[u][:, j, :], ht[:, u, m, j * P:(j + 1) * P], w2[:, m, :], start=(m == 0), stop=False)
                        mm = pe.matmul(ps_f[u][:, j, :], g.ones[0:1, :], b2[:, :], start=False, stop=True)
                    mm.then_inc(f_done, 1)

                def body(k, first):
                    for u in range(2):
                        gi = 2 * k + u
                        pe.wait_ge(loaded[u], 16 * k + 16)
                        for i in range(4):
                            if not (first and u == 0):
                                pe.wait_ge(h_kept, 4 * gi + i - 3)
                            for m in (2 * i, 2 * i + 1):
                                for c in range(KC):
                                    mm = pe.matmul(ps_h[i][:, m % 2, :], w1[:, c, m * P:(m + 1) * P], chunk(xt, u, c), start=(c == 0), stop=(c == KC - 1))
                            mm.then_inc(h_done, 1)
                        if not (first and u == 0):
                            last(gi - 1, 1 - u, first)
                peeled(pe, PAIRS, body)
                last(GROUPS - 1, 1, False)

            @block.scalar
            def _(act):
                act.wait_ge(w_loaded, 64)

                def body(k, first):
                    for u in range(2):
                        gi = 2 * k + u
                        if not first:
                            act.wait_ge(f_done, gi - 1)
                        for i in range(4):
                            act.wait_ge(h_done, 4 * gi + i + 1)
                            for m in (2 * i, 2 * i + 1):
                                op = act.activation(ht[:, u, m, :], ps_h[i][:, m % 2, :], ACT.Gelu_apprx_tanh, bias=b1[:, m:m + 1])
                            op.then_inc(h_kept, 1)
                        act.sem_inc(used, 1)
                peeled(act, PAIRS, body)

            @block.vector
            def _(dve):
                def body(k, first):
                    for u in range(2):
                        gi = 2 * k + u
                        dve.wait_ge(f_done, gi + 1)
                        for j in range(GROUP):
                            at = x_block(g, gi * GROUP + j)
                            op = dve.scalar_tensor_tensor(at, ps_f[u][:, j, :], col(g.gain, gi * GROUP + j), at, ALU.mult, ALU.add)
                        op.then_inc(added, 1)
                peeled(dve, PAIRS, body)


def layer0_steps(nc, g):
    return [
        lambda: load_inputs(nc, g),
        lambda: item_tables(nc, g),
        lambda: normalize(nc, g, "norm0", g.xn_rows, g.xn_turned, second=g.rstd2),
        lambda: aggregate0(nc, g),
        lambda: key_max(nc, g),
        lambda: context0(nc, g),
        lambda: mix0(nc, g),
        lambda: normalize(nc, g, "norm1", None, g.xn_turned, narrow=(g.given["L0_ffn_gW"], g.logits)),
        lambda: expert_weights(nc, g),
        lambda: ffn0(nc, g),
    ]


def layer1_steps(nc, g):
    return [
        lambda: normalize(nc, g, "norm2", g.xn_rows, g.xn_turned),
        lambda: edge_steps(nc, g),
        lambda: gather_steps(nc, g),
        lambda: finish_gnn(nc, g),
        lambda: normalize(nc, g, "norm3", None, g.xn_turned, narrow=(g.given["L1_ffn_wr"], g.router), add_back=True),
        lambda: select(nc, g),
        lambda: ffn1(nc, g),
    ]


def edge_steps(nc, g):
    with (nc.sbuf_tensor("terms", [P, TILES, 2 * GAT_HEADS], F32) as g.terms,
          nc.sbuf_tensor("first_edge", [P, NODE_BLOCKS], U32) as g.first_edge,
          nc.sbuf_tensor("last_edge", [P, NODE_BLOCKS], U32) as g.last_edge,
          nc.sbuf_tensor("no_edge", [P, NODE_BLOCKS], F32) as g.no_edge,
          nc.sbuf_tensor("node_vals", [P, NODE_BLOCKS, GAT_HEADS], F32) as g.node_vals):
        node_tables(nc, g)
        edge_ranges(nc, g)
        with nc.sbuf_tensor("kv", [P, KC, P], F32) as g.kv, nc.sbuf_tensor("ks", [P, KC, P], F32) as g.ks:
            context1(nc, g)
            mix1(nc, g)
        attention(nc, g)


def gather_steps(nc, g):
    with nc.sbuf_tensor("ee_item", [P, ITEM_COLS, GAT_HEADS], F32) as g.ee_item:
        edge_items(nc, g)
        own_rows(nc, g)
        aggregate1(nc, g)


class Globals:
    pass


def build(nc, inputs, out, upto=99):
    g = Globals()
    g.given = inputs
    g.out = out

    def dram(name, shape, dt=F32):
        return nc.dram_tensor(name, shape, dt, kind="Internal").ap()

    g.srcP = dram("srcP", [EDGE_TILES, P], I32)
    g.dstP = dram("dstP", [EDGE_TILES, P], I32)
    g.wP = dram("wP", [EDGE_TILES, P])
    g.dst_terms = dram("dst_terms", [PAD_EDGES, GAT_HEADS])
    g.max_terms = dram("max_terms", [PAD_EDGES, GAT_HEADS])
    g.edge_terms = dram("edge_terms", [P, PER * GAT_HEADS])
    g.runs = dram("runs", [PAD_EDGES, GAT_HEADS])
    g.ee_rows = dram("ee_rows", [EDGE_TILES, P * GAT_HEADS])
    g.src_terms = dram("src_terms", [PAD_NODES, GAT_HEADS])
    g.node_rows = dram("node_rows", [PAD_NODES, 2 * C])
    g.own = dram("own", [NODE_BLOCKS * P, C + GAT_HEADS])
    g.sums = dram("sums", [NODE_BLOCKS * P, 2 * C + GAT_HEADS])
    g.code_row = dram("code_row", [ITEM_COLS], I32)
    g.xn_rows = dram("xn_rows", [PAD_NODES, C])
    g.xn_turned = dram("xn_turned", [GROUPS, P, KC * ROWS])
    with ExitStack() as ctx:
        def sb(name, shape, dt=F32):
            return ctx.enter_context(nc.sbuf_tensor(name, shape, dt))
        g.x_sb = sb("x_sb", [P, TILES, C])
        g.iota = sb("iota", [P, P])
        g.part = sb("part", [P, 1])
        g.node0 = sb("node0", [P, TILES])
        g.ident = sb("ident", [P, P])
        g.same_head = sb("same_head", [P, P])
        g.half = sb("half", [P, 2, P])
        g.upper = sb("upper", [P, P])
        g.ones = sb("ones", [P, P])
        g.ones_bf = sb("ones_bf", [P, P], BF16)
        g.zrow_bf = sb("zrow_bf", [1, 288], BF16)
        g.zrow = sb("zrow", [1, 288])
        g.maskcol = sb("maskcol", [P, TILES])
        g.maskbias = sb("maskbias", [P, TILES])
        g.deg_cnt = sb("deg_cnt", [P, NODE_BLOCKS, 2])
        g.item_code = sb("item_code", [1, ITEM_COLS], I32)
        g.tile_of = sb("tile_of", [P, ITEM_GROUPS], U32)
        g.src_item = sb("src_item", [P, ITEM_COLS], U16)
        g.dst_item = sb("dst_item", [P, ITEM_COLS])
        g.w_item = sb("w_item", [P, ITEM_COLS])
        with ExitStack() as ctx0:
            def sb0(name, shape, dt=F32):
                return ctx0.enter_context(nc.sbuf_tensor(name, shape, dt))
            g.wqc = sb0("wqc", [P, KC, C])
            g.k_shift = sb0("k_shift", [P, C])
            g.logits = sb0("logits", [P, TILES, EXPERTS])
            g.mix5 = sb0("mix5", [P, TILES, EXPERTS + 1])
            g.rstd2 = sb0("rstd2", [P, TILES])
            for step in layer0_steps(nc, g)[:upto]:
                step()
        if upto > 10:
            g.dinv = sb("dinv", [P, TILES])
            g.self_ee = sb("self_ee", [P, NODE_BLOCKS, GAT_HEADS])
            g.router = sb("router", [P, TILES, 1])
            g.gain = sb("gain", [P, TILES])
            for step in layer1_steps(nc, g)[:upto - 10]:
                step()
        store_out(nc, g)


def store_out(nc, g):
    with phase(nc, "store") as ph:
        stored = ph.sem("stored")
        with nc.Block() as block:
            @block.sync
            def _(sp):
                to = g.out[0:FULL_TILES * P, :].rearrange("(t p) c -> p t c", p=P)
                cuts = [0, 16, 32, 48, 64, 80, FULL_TILES]
                for a, b in zip(cuts[:-1], cuts[1:]):
                    sp.dma_start(to[:, a:b, :], g.x_sb[:, a:b, :]).then_inc(stored, 16)
                sp.dma_start(g.out[FULL_TILES * P:NODES, :], g.x_sb[0:TAIL, FULL_TILES, :]).then_inc(stored, 16)
                sp.wait_ge(stored, 16 * len(cuts))


def kernel(**inputs):
    import numpy as _np
    import concourse.bacc as _bacc
    from concourse import mybir as _mybir
    from concourse.bass_utils import run_bass_kernel_spmd as _run

    nc = _bacc.Bacc("TRN2", target_bir_lowering=False, num_devices=1)
    arrays, aps = {}, {}
    for name, value in inputs.items():
        a = _np.ascontiguousarray(value)
        arrays[f"in_{name}_dram"] = a
        aps[name] = nc.dram_tensor(f"in_{name}_dram", a.shape, _mybir.dt.from_np(a.dtype), kind="ExternalInput").ap()
    out = nc.dram_tensor("out_0_dram", (NODES, C), F32, kind="ExternalOutput").ap()
    build(nc, aps, out)
    r = _run(nc, [arrays], core_ids=[0])
    return r.results[0]["out_0_dram"]
```
